# Optimizing a Trainium2 kernel written in Bass

```python
import numpy as np
import jax
import jax.numpy as jnp

def _softmax(x, axis=-1):
    return jax.nn.softmax(x, axis=axis)

def _gelu(x):
    return jax.nn.gelu(x, approximate=True)

def _silu(x):
    return jax.nn.silu(x)

def _sigmoid(x):
    return jax.nn.sigmoid(x)

def _layernorm(x, axis=-1, eps=1e-05):
    m = jnp.mean(x, axis=axis, keepdims=True)
    v = jnp.var(x, axis=axis, keepdims=True)
    return (x - m) / jnp.sqrt(v + eps)

def _scatter_add(tgt, idx, src, axis=0):
    return tgt.at[idx].add(src)

def _segment_sum(src, seg, n):
    return jax.ops.segment_sum(src, seg, n)
kernel_name = 'mk_seq_postln_d2_jaxref_r8_347a53'

def setup_inputs(seed: int=0):
    np.random.seed(seed)
    _w = jnp.asarray

    def _L0_attn_setup():
        import jax, jax.numpy as jnp
        import numpy as np
        N_HEAD = 16
        BUCKET = 64
        HIDDEN = 128
        EPS = 1e-05

        def _ln(x, g, b):
            m = x.mean(-1, keepdims=True)
            v = x.var(-1, keepdims=True)
            return (x - m) * jax.lax.rsqrt(v + EPS) * g + b
        key = jax.random.key(seed)
        ks = jax.random.split(key, 6)

        def w(k, shape, s=0.02):
            return jax.random.normal(k, shape, jnp.float32) * s
        C = HIDDEN
        return {'x': jax.random.normal(ks[0], (4, 1024, C), jnp.float32), 'ln1_g': jnp.ones((C,), jnp.float32), 'ln1_b': jnp.zeros((C,), jnp.float32), 'w_qkv': w(ks[1], (C, 3 * C)), 'b_qkv': jnp.zeros((3 * C,), jnp.float32), 'w_out': w(ks[2], (C, C)), 'b_out': jnp.zeros((C,), jnp.float32), 'ln2_g': jnp.ones((C,), jnp.float32), 'ln2_b': jnp.zeros((C,), jnp.float32), 'w1': w(ks[3], (C, 4 * C)), 'b1': jnp.zeros((4 * C,), jnp.float32), 'w2': w(ks[4], (4 * C, C)), 'b2': jnp.zeros((C,), jnp.float32)}
    _L0_attn_in = _L0_attn_setup()

    def _L0_ffn_setup():
        import jax, jax.numpy as jnp
        import numpy as np
        B, L, D = (4, 128, 128)
        E, H = (8, 512)
        CAPACITY = 6
        key = jax.random.key(seed)
        ks = jax.random.split(key, 6)
        x = jax.random.normal(ks[0], (B, L, D), dtype=jnp.float32)
        gate_weight = jax.random.normal(ks[1], (E, D), dtype=jnp.float32) * 0.006
        w1 = jax.random.normal(ks[2], (E, H, D), dtype=jnp.float32) * 0.02
        b1 = jnp.zeros((E, H), dtype=jnp.float32)
        w2 = jax.random.normal(ks[3], (E, D, H), dtype=jnp.float32) * 0.02
        b2 = jnp.zeros((E, D), dtype=jnp.float32)
        return {'x': x, 'gate_weight': gate_weight, 'w1': w1, 'b1': b1, 'w2': w2, 'b2': b2}
    _L0_ffn_in = _L0_ffn_setup()

    def _L1_attn_setup():
        import jax, jax.numpy as jnp
        import numpy as np
        HEADS = 16
        LOCAL_HEADS = 4
        DIM = 128
        DH = DIM // HEADS
        WINDOW = 128
        BLINDSPOT = 64

        def _look_around(x, buckets):
            pad_cfg = ((0, 0), (1, 0)) + ((0, 0),) * (x.ndim - 2)
            pv = -1.0 if jnp.issubdtype(x.dtype, jnp.floating) else -1
            p = jnp.pad(x, pad_cfg, constant_values=pv)
            return jnp.concatenate([p[:, :buckets], p[:, 1:buckets + 1]], axis=2)

        def _local_attn(q, k, v):
            b, lh, t, e = q.shape
            bm = b * lh
            buckets = t // WINDOW
            bq = q.reshape(bm, buckets, WINDOW, e)
            bk = k.reshape(bm, buckets, WINDOW, e)
            bv = v.reshape(bm, buckets, WINDOW, e)
            bk2 = _look_around(bk, buckets)
            bv2 = _look_around(bv, buckets)
            ticker = jnp.arange(t, dtype=jnp.int32).reshape(1, buckets, WINDOW)
            bq_k = _look_around(ticker, buckets)
            dots = jnp.einsum('buie,buje->buij', bq, bk2) * e ** (-0.5)
            mask_value = -jnp.finfo(dots.dtype).max
            causal_mask = ticker[:, :, :, None] < bq_k[:, :, None, :]
            pad_mask = bq_k[:, :, None, :] == -1
            dots = jnp.where(causal_mask | pad_mask, mask_value, dots)
            attn = jax.nn.softmax(dots, axis=-1)
            out = jnp.einsum('buij,buje->buie', attn, bv2)
            return out.reshape(b, lh, t, e)

        def _causal_linear_attn(q, k, v):
            b, h, n, e = q.shape
            u = n // BLINDSPOT
            q = jax.nn.softmax(q, axis=-1)
            k = jax.nn.elu(k) + 1.0
            bq = q.reshape(b, h, u, BLINDSPOT, e)
            bk = k.reshape(b, h, u, BLINDSPOT, e)
            bv = v.reshape(b, h, u, BLINDSPOT, e)
            bk_cumsum = jnp.cumsum(bk.sum(axis=-2), axis=-2)
            ctx = jnp.einsum('bhund,bhune->bhude', bk, bv)
            ctx = jnp.cumsum(ctx, axis=2)
            ctx = ctx / (bk_cumsum[..., None] + 1e-06)
            ctx = jnp.pad(ctx, ((0, 0), (0, 0), (1, 0), (0, 0), (0, 0)))[:, :, :u]
            attn = jnp.einsum('bhund,bhude->bhune', bq, ctx)
            return attn.reshape(b, h, n, e)
        key = jax.random.key(seed)
        ks = jax.random.split(key, 6)
        s = 1.0 / np.sqrt(DIM)
        x = jax.random.normal(ks[0], (4, 1024, DIM), dtype=jnp.float32)
        Wq = jax.random.normal(ks[1], (DIM, DIM), dtype=jnp.float32) * s
        Wk = jax.random.normal(ks[2], (DIM, DIM), dtype=jnp.float32) * s
        Wv = jax.random.normal(ks[3], (DIM, DIM), dtype=jnp.float32) * s
        Wo = jax.random.normal(ks[4], (DIM, DIM), dtype=jnp.float32) * s
        bo = jax.random.normal(ks[5], (DIM,), dtype=jnp.float32) * 0.01
        return {'x': x, 'Wq': Wq, 'Wk': Wk, 'Wv': Wv, 'Wo': Wo, 'bo': bo}
    _L1_attn_in = _L1_attn_setup()

    def _L1_ffn_setup():
        import jax, jax.numpy as jnp
        import numpy as np
        TOP_K = 2
        key = jax.random.key(seed)
        ks = jax.random.split(key, 6)
        B, S, D, F, E = (2, 256, 128, 512, 8)
        sd = 1.0 / np.sqrt(D)
        sf = 1.0 / np.sqrt(F)
        return {'x': jax.random.normal(ks[0], (B, S, D), jnp.float32), 'gate_w': jax.random.normal(ks[1], (D, E), jnp.float32) * sd, 'w1': jax.random.normal(ks[2], (E, D, F), jnp.float32) * sd, 'b1': jax.random.normal(ks[3], (E, F), jnp.float32) * 0.01, 'w2': jax.random.normal(ks[4], (E, F, D), jnp.float32) * sf, 'b2': jax.random.normal(ks[5], (E, D), jnp.float32) * 0.01}
    _L1_ffn_in = _L1_ffn_setup()
    _d = {'L0_attn_x': _L0_attn_in['x'], 'L0_attn_ln1_g': _L0_attn_in['ln1_g'], 'L0_attn_ln1_b': _L0_attn_in['ln1_b'], 'L0_attn_w_qkv': _L0_attn_in['w_qkv'], 'L0_attn_b_qkv': _L0_attn_in['b_qkv'], 'L0_attn_w_out': _L0_attn_in['w_out'], 'L0_attn_b_out': _L0_attn_in['b_out'], 'L0_attn_ln2_g': _L0_attn_in['ln2_g'], 'L0_attn_ln2_b': _L0_attn_in['ln2_b'], 'L0_attn_w1': _L0_attn_in['w1'], 'L0_attn_b1': _L0_attn_in['b1'], 'L0_attn_w2': _L0_attn_in['w2'], 'L0_attn_b2': _L0_attn_in['b2'], 'L0_ffn_gate_weight': _L0_ffn_in['gate_weight'], 'L0_ffn_w1': _L0_ffn_in['w1'], 'L0_ffn_b1': _L0_ffn_in['b1'], 'L0_ffn_w2': _L0_ffn_in['w2'], 'L0_ffn_b2': _L0_ffn_in['b2'], 'L1_attn_Wq': _L1_attn_in['Wq'], 'L1_attn_Wk': _L1_attn_in['Wk'], 'L1_attn_Wv': _L1_attn_in['Wv'], 'L1_attn_Wo': _L1_attn_in['Wo'], 'L1_attn_bo': _L1_attn_in['bo'], 'L1_ffn_gate_w': _L1_ffn_in['gate_w'], 'L1_ffn_w1': _L1_ffn_in['w1'], 'L1_ffn_b1': _L1_ffn_in['b1'], 'L1_ffn_w2': _L1_ffn_in['w2'], 'L1_ffn_b2': _L1_ffn_in['b2']}
    _x0 = _d['L0_attn_x']
    _d['L0_attn_x'] = jax.random.normal(jax.random.fold_in(jax.random.key(seed), 1), (16, 256, 128), dtype=_x0.dtype)
    del _x0
    return _d

def reference(L0_attn_x, L0_attn_ln1_g, L0_attn_ln1_b, L0_attn_w_qkv, L0_attn_b_qkv, L0_attn_w_out, L0_attn_b_out, L0_attn_ln2_g, L0_attn_ln2_b, L0_attn_w1, L0_attn_b1, L0_attn_w2, L0_attn_b2, L0_ffn_gate_weight, L0_ffn_w1, L0_ffn_b1, L0_ffn_w2, L0_ffn_b2, L1_attn_Wq, L1_attn_Wk, L1_attn_Wv, L1_attn_Wo, L1_attn_bo, L1_ffn_gate_w, L1_ffn_w1, L1_ffn_b1, L1_ffn_w2, L1_ffn_b2):

    def _L0_attn_ref(x, ln1_g, ln1_b, w_qkv, b_qkv, w_out, b_out, ln2_g, ln2_b, w1, b1, w2, b2):
        import jax, jax.numpy as jnp
        import numpy as np
        N_HEAD = 16
        BUCKET = 64
        HIDDEN = 128
        EPS = 1e-05

        def _ln(x, g, b):
            m = x.mean(-1, keepdims=True)
            v = x.var(-1, keepdims=True)
            return (x - m) * jax.lax.rsqrt(v + EPS) * g + b
        B, T, C = x.shape
        nb = T // BUCKET
        hd = C // N_HEAD
        scale = 1.0 / np.sqrt(hd)
        h = _ln(x, ln1_g, ln1_b)
        qkv = h @ w_qkv + b_qkv
        q, k, v = jnp.split(qkv, 3, axis=-1)

        def buck(t):
            return t.reshape(B, nb, BUCKET, N_HEAD, hd)
        qb, kb, vb = (buck(q), buck(k), buck(v))
        kp = jnp.concatenate([jnp.zeros_like(kb[:, :1]), kb[:, :-1]], axis=1)
        vp = jnp.concatenate([jnp.zeros_like(vb[:, :1]), vb[:, :-1]], axis=1)
        kc = jnp.concatenate([kp, kb], axis=2)
        vc = jnp.concatenate([vp, vb], axis=2)
        scores = jnp.einsum('bnihd,bnjhd->bnhij', qb, kc) * scale
        i = jnp.arange(BUCKET)[:, None]
        j = jnp.arange(2 * BUCKET)[None, :]
        mask = (j < BUCKET) | (j - BUCKET <= i)
        scores = jnp.where(mask, scores, -jnp.inf)
        attn = jax.nn.softmax(scores, axis=-1)
        ob = jnp.einsum('bnhij,bnjhd->bnihd', attn, vc).reshape(B, T, C)
        x = x + ob @ w_out + b_out
        h2 = _ln(x, ln2_g, ln2_b)
        m = jax.nn.gelu(h2 @ w1 + b1, approximate=False) @ w2 + b2
        return x + m

    def _L0_ffn_ref(x, gate_weight, w1, b1, w2, b2):
        import jax, jax.numpy as jnp
        import numpy as np
        B, L, D = (4, 128, 128)
        E, H = (8, 512)
        CAPACITY = 6
        logits = jnp.einsum('bld,ed->ble', x, gate_weight)
        expert_k = B * L * CAPACITY
        kth_val = jnp.sort(logits.reshape(-1))[expert_k - 1]
        mask = (logits >= kth_val).astype(x.dtype)
        gates = logits * mask
        h = jax.nn.gelu(jnp.einsum('bld,ehd->bleh', x, w1) + b1, approximate=True)
        y = jnp.einsum('bleh,edh->blde', h, w2) + b2.T[None, None]
        out = jnp.einsum('blde,ble->bld', y, gates)
        return out

    def _L1_attn_ref(x, Wq, Wk, Wv, Wo, bo):
        import jax, jax.numpy as jnp
        import numpy as np
        HEADS = 16
        LOCAL_HEADS = 4
        DIM = 128
        DH = DIM // HEADS
        WINDOW = 128
        BLINDSPOT = 64

        def _look_around(x, buckets):
            pad_cfg = ((0, 0), (1, 0)) + ((0, 0),) * (x.ndim - 2)
            pv = -1.0 if jnp.issubdtype(x.dtype, jnp.floating) else -1
            p = jnp.pad(x, pad_cfg, constant_values=pv)
            return jnp.concatenate([p[:, :buckets], p[:, 1:buckets + 1]], axis=2)

        def _local_attn(q, k, v):
            b, lh, t, e = q.shape
            bm = b * lh
            buckets = t // WINDOW
            bq = q.reshape(bm, buckets, WINDOW, e)
            bk = k.reshape(bm, buckets, WINDOW, e)
            bv = v.reshape(bm, buckets, WINDOW, e)
            bk2 = _look_around(bk, buckets)
            bv2 = _look_around(bv, buckets)
            ticker = jnp.arange(t, dtype=jnp.int32).reshape(1, buckets, WINDOW)
            bq_k = _look_around(ticker, buckets)
            dots = jnp.einsum('buie,buje->buij', bq, bk2) * e ** (-0.5)
            mask_value = -jnp.finfo(dots.dtype).max
            causal_mask = ticker[:, :, :, None] < bq_k[:, :, None, :]
            pad_mask = bq_k[:, :, None, :] == -1
            dots = jnp.where(causal_mask | pad_mask, mask_value, dots)
            attn = jax.nn.softmax(dots, axis=-1)
            out = jnp.einsum('buij,buje->buie', attn, bv2)
            return out.reshape(b, lh, t, e)

        def _causal_linear_attn(q, k, v):
            b, h, n, e = q.shape
            u = n // BLINDSPOT
            q = jax.nn.softmax(q, axis=-1)
            k = jax.nn.elu(k) + 1.0
            bq = q.reshape(b, h, u, BLINDSPOT, e)
            bk = k.reshape(b, h, u, BLINDSPOT, e)
            bv = v.reshape(b, h, u, BLINDSPOT, e)
            bk_cumsum = jnp.cumsum(bk.sum(axis=-2), axis=-2)
            ctx = jnp.einsum('bhund,bhune->bhude', bk, bv)
            ctx = jnp.cumsum(ctx, axis=2)
            ctx = ctx / (bk_cumsum[..., None] + 1e-06)
            ctx = jnp.pad(ctx, ((0, 0), (0, 0), (1, 0), (0, 0), (0, 0)))[:, :, :u]
            attn = jnp.einsum('bhund,bhude->bhune', bq, ctx)
            return attn.reshape(b, h, n, e)
        b, t, dim = x.shape
        q = x @ Wq
        k = x @ Wk
        v = x @ Wv
        mh = lambda z: z.reshape(b, t, HEADS, DH).transpose(0, 2, 1, 3)
        q, k, v = (mh(q), mh(k), mh(v))
        lq, gq = (q[:, :LOCAL_HEADS], q[:, LOCAL_HEADS:])
        lk, gk = (k[:, :LOCAL_HEADS], k[:, LOCAL_HEADS:])
        lv, gv = (v[:, :LOCAL_HEADS], v[:, LOCAL_HEADS:])
        local_out = _local_attn(lq, lk, lv)
        global_out = _causal_linear_attn(gq, gk, gv)
        attn = jnp.concatenate([local_out, global_out], axis=1)
        attn = attn.transpose(0, 2, 1, 3).reshape(b, t, dim)
        return attn @ Wo + bo

    def _L1_ffn_ref(x, gate_w, w1, b1, w2, b2):
        import jax, jax.numpy as jnp
        import numpy as np
        TOP_K = 2
        B, S, D = x.shape
        T = B * S
        xf = x.reshape(T, D)
        gate_scores = jax.nn.softmax(xf @ gate_w, axis=-1)
        topk_scores, topk_idx = jax.lax.top_k(gate_scores, TOP_K)
        topk_scores = topk_scores / jnp.sum(topk_scores, axis=-1, keepdims=True)
        h = jax.nn.gelu(jnp.einsum('td,edf->etf', xf, w1) + b1[:, None, :], approximate=False)
        y = jnp.einsum('etf,efd->etd', h, w2) + b2[:, None, :]
        tok = jnp.arange(T)
        y_sel = y[topk_idx.T, tok[None, :]]
        out = jnp.einsum('kt,ktd->td', topk_scores.T, y_sel)
        return out.reshape(B, S, D)
    x = L0_attn_x
    x = _layernorm(x + _L0_attn_ref(x, L0_attn_ln1_g, L0_attn_ln1_b, L0_attn_w_qkv, L0_attn_b_qkv, L0_attn_w_out, L0_attn_b_out, L0_attn_ln2_g, L0_attn_ln2_b, L0_attn_w1, L0_attn_b1, L0_attn_w2, L0_attn_b2), axis=-1)
    x = _layernorm(x + _L0_ffn_ref(x, L0_ffn_gate_weight, L0_ffn_w1, L0_ffn_b1, L0_ffn_w2, L0_ffn_b2), axis=-1)
    x = _layernorm(x + _L1_attn_ref(x, L1_attn_Wq, L1_attn_Wk, L1_attn_Wv, L1_attn_Wo, L1_attn_bo), axis=-1)
    x = _layernorm(x + _L1_ffn_ref(x, L1_ffn_gate_w, L1_ffn_w1, L1_ffn_b1, L1_ffn_w2, L1_ffn_b2), axis=-1)
    return x

_drawn_inputs = setup_inputs


def setup_inputs(seed=0):
    import zlib

    import numpy as np

    out = dict(_drawn_inputs(seed))
    spreads = {'L0_attn_ln1_g': (1.0, 0.6),
     'L0_attn_ln1_b': (0.0, 0.457),
     'L0_attn_b_qkv': (0.0, 0.1),
     'L0_attn_b_out': (0.0, 0.1),
     'L0_attn_ln2_g': (1.0, 0.6),
     'L0_attn_ln2_b': (0.0, 0.337),
     'L0_attn_b1': (0.0, 0.1),
     'L0_attn_b2': (0.0, 0.1),
     'L0_ffn_b1': (0.0, 0.402),
     'L0_ffn_b2': (0.0, 0.1)}
    factors = {'L0_attn_w_qkv': 3.103, 'L1_ffn_b1': 8.0, 'L1_ffn_b2': 8.0}
    for name, (base, spread) in spreads.items():
        noise = np.random.default_rng([zlib.crc32(name.encode()), seed]).standard_normal(out[name].shape)
        drawn = base * np.exp(spread * noise) if base else spread * noise
        out[name] = jnp.asarray(drawn.astype(out[name].dtype))
    for name, factor in factors.items():
        out[name] = (out[name] * factor).astype(out[name].dtype)
    return out
```

```python
import concourse.bass as bass
from concourse import mybir
from contextlib import ExitStack

P = 128
NB, TB, C = 16, 256, 128
T = NB * TB
NT = T // P
H, HD = 16, 8
BK = 64
E, F = 8, 512
FB = F // P
CT = 512
NC_ = T // CT
EPS = 1e-5
NEG = -1e30
KEEP_FROM = 4 * 128 * 6

ALU = mybir.AluOpType
ACT = mybir.ActivationFunctionType
AX = mybir.AxisListType
F32 = mybir.dt.float32
F32R = mybir.dt.float32r
F16 = mybir.dt.float16
BF16 = mybir.dt.bfloat16
U32 = mybir.dt.uint32
ds = bass.ds


class Tally:

    def __init__(self, eng, sem, per, b):
        self.eng, self.sem, self.per, self.b, self.n = eng, sem, per, b, 0

    def inc(self, ins):
        ins.then_inc(self.sem, 1)
        self.n += 1

    def wait(self):
        self.eng.wait_ge(self.sem, self.b * self.per + self.n)

    def link(self, ins):
        self.inc(ins)
        self.wait()


class Turn:

    def __init__(self, i, off):
        self.n, self.p, self.half = i * 2 + off, off % 2, i + off // 2
        self.first = isinstance(i, int) and i * 2 + off < 1
        self.early = isinstance(i, int) and i * 2 + off < 2


def wait(eng, sem, value):
    if isinstance(value, int) and value <= 0:
        return
    eng.wait_ge(sem, value)


def settle(eng, passed):
    eng.sem_inc(passed, 1)


class Mem:

    def __init__(self, nc, ctx, tag):
        self.nc, self.ctx, self.tag, self.sems = nc, ctx, tag, []
        ctx.callback(self.clear)

    def clear(self):
        if self.sems:
            self.nc.clear_and_free_semaphores(self.sems)
            self.nc.all_engine_barrier()

    def sb(self, name, shape, dt=F32):
        return self.ctx.enter_context(self.nc.sbuf_tensor(f"{self.tag}__{name}", shape, dt))

    def ps(self, name, shape, dt=F32):
        return self.ctx.enter_context(self.nc.psum_tensor(f"{self.tag}__{name}", shape, dt))

    def sem(self, name):
        self.sems.append(self.nc.alloc_semaphore(f"{self.tag}__{name}"))
        return self.sems[-1]


def skewed(eng, n, step):
    step(Turn(0, 0), None, None)
    step(Turn(0, 1), Turn(0, 0), None)
    with eng.Fori(0, n // 2 - 1) as i:
        for off in (1, 2):
            step(Turn(i, off + 1), Turn(i, off), Turn(i, off - 1))
    last = n // 2 - 1
    step(None, Turn(last, 1), Turn(last, 0))
    step(None, None, Turn(last, 1))


ORDER_0 = [("scores", 0), ("scores", 1), ("output", 0), ("norm", 0), ("hT", 0), ("shift", 0),
           ("proj", 0), ("weights", 0), ("weights", 1), ("shift", 1), ("values", 0), ("weights", 2),
           ("values", 1), ("proj", 1), ("weights", 3), ("values", 2), ("weights", 4), ("values", 3),
           ("proj", 2), ("weights", 5), ("back", 0), ("values", 4), ("proj", 3), ("weights", 6),
           ("values", 5), ("vT", 0), ("weights", 7), ("values", 6), ("windows", 0), ("values", 7),
           ("back", 1)]


def attention_0(nc, d, keep):
    with ExitStack() as ctx:
        m = Mem(nc, ctx, "a")
        wq = m.sb("wq", [P, 4, P])
        wk = m.sb("wk", [P, 4, P])
        wv = m.sb("wv", [P, P])
        wo = m.sb("wo", [P, P])
        cols = m.sb("cols", [P, 16])
        bo = m.sb("bo", [P, P])
        ident = m.sb("ident", [P, P])
        ident16 = m.sb("ident16", [P, P], F16)
        identb = m.sb("identb", [P, P], BF16)
        causal = m.sb("causal", [P, 4, P], BF16)
        x = m.sb("x", [P, NT, C])
        xb = [m.sb(f"xb{p}", [P, 2, C]) for p in range(2)]
        st = m.sb("st", [P, 2, 6])
        mv = m.sb("mv", [P, 2, 2])
        half = m.sb("half", [P, 2])
        rstd = m.sb("rstd", [P, 2])
        hn = m.sb("hn", [P, 2, C])
        hT = m.sb("hT", [P, TB])
        full = m.sb("full", [P, 2, 2, TB])
        high = m.sb("high", [P, 2, 2, TB], F16)
        qs = [m.sb(f"qs{p}", [P, 4, TB], F16) for p in range(2)]
        ks = [m.sb(f"ks{p}", [P, 4, BK + TB], F16) for p in range(2)]
        vT = m.sb("vT", [P, BK + TB])
        va = [m.sb(f"va{p}", [P, 4, H, 32]) for p in range(2)]
        mx = m.sb("mx", [P, 2, 4, 4])
        mpad = m.sb("mpad", [P, 2, 4, 4, 32], F16)
        q2 = m.sb("q2", [P, 2, 4, P], F16)
        pt = m.sb("pt", [P, 4, 512])
        ots = m.sb("ots", [P, 2, 512])
        rc = m.sb("rc", [P, 2, H])
        ob = [m.sb(f"ob{p}", [P, 2, C]) for p in range(2)]
        aT = m.sb("aT", [P, TB])

        S = m.ps("S", [P, 2, 512])
        ST = m.ps("ST", [P, 2, 512])
        OT = m.ps("OT", [P, 512])
        MI = m.ps("MI", [P, 512])
        W1 = m.ps("W1", [P, 512])
        W3 = m.ps("W3", [P, 512])
        MT = MI[:, 0:256].bitcast(F16).rearrange("p (a b) -> p a b", a=4)

        loaded = m.sem("loaded")
        cleared = m.sem("cleared")
        x_first, x_rest = m.sem("x_first"), m.sem("x_rest")
        xb_done = m.sem("xb_done")
        ln = m.sem("ln")
        var_done = m.sem("var_done")
        rstd_done = m.sem("rstd_done")
        pool_ln = m.sem("pool_ln")
        passed_pool, passed_dve = m.sem("passed_pool"), m.sem("passed_dve")
        hn_done = m.sem("hn_done")
        w1_full = m.sem("w1_full")
        w1_free = m.sem("w1_free")
        high_done = m.sem("high_done")
        qk_done = m.sem("qk_done")
        s_full = m.sem("s_full")
        s_free = m.sem("s_free")
        mx_own = m.sem("mx_own")
        mpad_done = m.sem("mpad_done")
        mi_full = m.sem("mi_full")
        mi_free = m.sem("mi_free")
        st_full = m.sem("st_full")
        exp_done = m.sem("exp_done")
        causal_done = m.sem("causal_done")
        pv_done = m.sem("pv_done")
        ot_free = m.sem("ot_free")
        norm_own = m.sem("norm_own")
        o_done = m.sem("o_done")
        w3_full = m.sem("w3_full")
        w3_free = m.sem("w3_free")
        x1_own = m.sem("x1_own")
        x1_done = m.sem("x1_done")
        LOADS = 14

        def rows_landed(eng, turn):
            eng.wait_ge(x_first if isinstance(turn.n, int) and turn.n < 2 else x_rest, 16)

        def rows(turn, a):
            return x[:, ds(turn.n * 2 + a, 1), :].rearrange("p a c -> p (a c)")

        g1, s1 = cols[:, 0:1], cols[:, 1:2]
        scale = float(HD) ** -0.5
        block = ctx.enter_context(nc.Block())

        @block.sync
        def _(sp):
            sp.dma_start(x[:, 0:4, :], d["x"][:, 0:4, :]).then_inc(x_first, 16)
            for dst, src in ((wq[:], d["w_q"]), (wk[:], d["w_k"]), (wv[:], d["w_v"]), (wo[:], d["w_out"]),
                             (cols[:], d["cols"]), (ident[:], d["ident"]), (ident16[:], d["ident16"]),
                             (identb[:], d["identb"]), (causal[:], d["causal64"]),
                             (bo[:], d["b_out"].to_broadcast([P, C])),
                             (ks[0][:, :, 0:BK], d["kpad"]), (ks[1][:, :, 0:BK], d["kpad"]),
                             (keep["ident"][:], d["ident"]), (keep["gate0"][:], d["gate0"])):
                sp.dma_start(dst, src).then_inc(loaded, 16)
            sp.dma_start(x[:, 4:NT, :], d["x"][:, 4:NT, :]).then_inc(x_rest, 16)

        @block.gpsimd
        def _(pool):
            pool.memset(half[:], -0.5)
            pool.memset(va[0][:], 0.0)
            pool.memset(va[1][:], 0.0)
            pool.memset(vT[:], 0.0)
            pool.memset(mpad[:], 0.0).then_inc(cleared, 1)
            pool.wait_ge(cleared, 1)
            for v in va:
                pool.memset(v[:, :, :, HD:HD + 1], 1.0).then_inc(cleared, 1)
            pool.wait_ge(cleared, 3)
            pool.wait_ge(loaded, 16 * LOADS)

            def step(pre, main, post):
                for what, k in ORDER_0:
                    if what == "norm" and pre:
                        pool.wait_ge(var_done, pre.n + 1)
                        settle(pool, passed_pool)
                        t = Tally(pool, pool_ln, 1, pre.n)
                        t.link(pool.tensor_scalar(rstd[:], mv[:, :, 1], EPS, 1.0, ALU.add, ALU.mult))
                        pool.tensor_tensor(rstd[:], rstd[:], half[:], ALU.pow).then_inc(rstd_done, 1)
                        rows_landed(pool, pre)
                        wait(pool, x1_done, 0 if pre.early else pre.n - 1)
                        for t in range(2):
                            ins = pool.tensor_tensor(xb[pre.p][:, t, :], rows(pre, t), bo[:], ALU.add)
                        ins.then_inc(xb_done, 1)
                    if what == "proj" and pre:
                        pool.wait_ge(w1_free, pre.n * 7 + 2 + k)
                        settle(pool, passed_pool)
                        pool.tensor_copy(high[:, k % 2], full[:, k % 2]).then_inc(high_done, 1)
                    if what == "weights" and main:
                        pool.wait_ge(exp_done, main.n * 8 + k + 1)
                        settle(pool, passed_pool)
                        v = pt[:, k % 4, :].rearrange("p (a i) -> p a i", a=8)
                        pool.affine_select(out=v, in_=v, compare_op=ALU.is_ge, fill=0.0, base=BK,
                                           pattern=[[0, 8], [1, BK]],
                                           channel_multiplier=-1).then_inc(causal_done, 1)

            skewed(pool, NB, step)

        @block.scalar
        def _(act):
            act.wait_ge(loaded, 16 * LOADS)
            act.wait_ge(cleared, 3)

            def step(pre, main, post):
                for what, k in ORDER_0:
                    if what == "hT" and pre:
                        act.wait_ge(w1_full, pre.n * 7 + 1)
                        act.activation(hT[:], W1[:, 0:TB], ACT.Identity, scale=g1, bias=s1).then_inc(w1_free, 1)
                    if what == "proj" and pre:
                        act.wait_ge(w1_full, pre.n * 7 + 2 + k)
                        if not (pre.first and k < 2):
                            act.wait_ge(qk_done, pre.n * 4 + k - 1)
                        for a in range(2):
                            c = 2 + 2 * k + a
                            ins = act.activation(full[:, k % 2, a, :], W1[:, a * TB:(a + 1) * TB],
                                                 ACT.Identity, bias=cols[:, c:c + 1])
                        ins.then_inc(w1_free, 1)
                    if what == "vT" and pre:
                        act.wait_ge(w1_full, pre.n * 7 + 6)
                        act.activation(vT[:, BK:BK + TB], W1[:, 0:TB], ACT.Identity,
                                       bias=cols[:, 10:11]).then_inc(w1_free, 1)
                    if what == "weights" and main:
                        act.wait_ge(st_full, main.n * 8 + k + 1)
                        if not (main.first and k < 4):
                            act.wait_ge(pv_done, main.n * 8 + k - 3)
                        act.activation(pt[:, k % 4, :], ST[:, k % 2, :], ACT.Exp,
                                       scale=scale).then_inc(exp_done, 1)
                    if what == "back" and main:
                        act.wait_ge(pv_done, main.n * 8 + 4 * k + 4)
                        if not main.first:
                            act.wait_ge(mi_full, main.n * 4 - 1 + k)
                        act.activation(ots[:, k, :], OT[:], ACT.Copy).then_inc(ot_free, 1)
                    if what == "output" and post:
                        act.wait_ge(w3_full, post.n * 2 + 1)
                        act.activation(aT[:], W3[:, 0:TB], ACT.Copy).then_inc(w3_free, 1)

            skewed(act, NB, step)

        @block.vector
        def _(dve):
            dve.wait_ge(loaded, 16 * LOADS)
            dve.wait_ge(cleared, 3)

            def step(pre, main, post):
                for what, k in ORDER_0:
                    if what == "norm" and pre:
                        rows_landed(dve, pre)
                        t = Tally(dve, ln, 4, pre.n)
                        for a in range(2):
                            t.inc(dve.bn_stats(st[:, a, :], rows(pre, a)))
                        t.wait()
                        settle(dve, passed_dve)
                        t.inc(dve.bn_aggr(mv[:, 0, :], st[:, 0, :]))
                        dve.bn_aggr(mv[:, 1, :], st[:, 1, :]).then_inc(var_done, 1)
                        wait(dve, w1_full, 0 if pre.first else pre.n * 7 - 6)
                        dve.wait_ge(rstd_done, pre.n + 1)
                        t.inc(dve.tensor_scalar(hn[:, 0, :], rows(pre, 0), mv[:, 0, 0:1], rstd[:, 0:1],
                                                ALU.subtract, ALU.mult))
                        dve.tensor_scalar(hn[:, 1, :], rows(pre, 1), mv[:, 1, 0:1], rstd[:, 1:2],
                                          ALU.subtract, ALU.mult).then_inc(hn_done, 1)
                    if what == "proj" and pre:
                        dve.wait_ge(high_done, pre.n * 4 + k + 1)
                        wait(dve, st_full, 0 if pre.early else (pre.n - 1) * 8)
                        out = (qs[pre.p][:, 2 * k:2 * k + 2, :] if k < 2 else
                               ks[pre.p][:, 2 * k - 4:2 * k - 2, BK:BK + TB])
                        low = cols[:, 11:12] if k < 2 else cols[:, 12:13]
                        dve.scalar_tensor_tensor(out=out, in0=high[:, k % 2], scalar=low, in1=full[:, k % 2],
                                                 op0=ALU.mult, op1=ALU.add).then_inc(qk_done, 1)
                    if what == "windows" and pre:
                        dve.wait_ge(w1_full, pre.n * 7 + 7)
                        wait(dve, pv_done, 0 if pre.early else (pre.n - 1) * 8)
                        for w in range(4):
                            ins = dve.tensor_copy(va[pre.p][:, w, :, 0:HD],
                                                  W1[:, w * P:(w + 1) * P].rearrange("p (h e) -> p h e", h=H))
                        ins.then_inc(w1_free, 1)
                    if what == "scores" and main:
                        for g in range(4):
                            u = 4 * k + g
                            dve.wait_ge(s_full, main.n * 8 + u + 1)
                            dve.tensor_reduce(mx[:, k, :, g], S[:, u % 2, :].rearrange("p (a j) -> p a j", a=4),
                                              AX.X, ALU.max).then_inc(s_free, 1)
                        dve.wait_ge(s_free, main.n * 8 + 4 * k + 4)
                        wait(dve, mi_full, 0 if main.first else main.n * 4 - 3 + k)
                        t = Tally(dve, mx_own, 2, main.n)
                        t.n = k
                        t.link(dve.tensor_copy(mpad[:, k, :, :, 24], mx[:, k]))
                        dve.tensor_tensor(mpad[:, k, :, :, 25], mx[:, k], mpad[:, k, :, :, 24],
                                          ALU.subtract).then_inc(mpad_done, 1)
                    if what == "shift" and main:
                        dve.wait_ge(mi_full, main.n * 4 + k + 1)
                        wait(dve, st_full, 0 if main.first else main.n * 8 - 4 + 4 * k)
                        dve.tensor_tensor(q2[:, k], qs[main.p][:, :, k * P:(k + 1) * P], MT,
                                          ALU.subtract).then_inc(mi_free, 1)
                    if what == "back" and main:
                        o4 = MI[:].rearrange("p (h e) -> p h e", e=32)
                        dve.wait_ge(mi_full, main.n * 4 + 3 + k)
                        t = Tally(dve, norm_own, 2, main.n)
                        t.n = k
                        t.link(dve.reciprocal(rc[:, k, :], o4[:, :, HD]))
                        wait(dve, w3_full, 0 if main.early else main.n * 2 - 2)
                        ins = dve.tensor_tensor(ob[main.p][:, k, :].rearrange("p (h e) -> p h e", h=H),
                                                o4[:, :, 0:HD], rc[:, k, :, None].to_broadcast([P, H, HD]),
                                                ALU.mult)
                        ins.then_inc(mi_free, 1)
                    if what == "output" and post:
                        dve.wait_ge(w3_full, post.n * 2 + 2)
                        dve.wait_ge(xb_done, post.n + 1)
                        t = Tally(dve, x1_own, 1, post.n)
                        x1 = keep["x1"][:, ds(post.n * 2, 2), :]
                        t.inc(dve.tensor_tensor(x1, W3[:, 0:TB].rearrange("p (t c) -> p t c", t=2),
                                                xb[post.p][:], ALU.add))
                        t.wait()
                        ins = dve.tensor_tensor(keep["xs"][:, ds(post.n * 2, 2), :], x1, x[:, ds(post.n * 2, 2), :], ALU.add)
                        ins.then_inc(x1_done, 1)

            skewed(dve, NB, step)

        @block.tensor
        def _(pe):
            pe.wait_ge(loaded, 16 * LOADS)
            pe.wait_ge(cleared, 3)

            def step(pre, main, post):
                def job1(k):
                    if not (pre.first and k == 0):
                        pe.wait_ge(w1_free, pre.n * 7 + k)

                for what, k in ORDER_0:
                    if what == "hT" and pre:
                        job1(0)
                        pe.wait_ge(hn_done, pre.n + 1)
                        for a in range(2):
                            ins = pe.transpose(W1[:, a * P:(a + 1) * P], hn[:, a, :], ident[:])
                        ins.then_inc(w1_full, 1)
                    if what == "proj" and pre:
                        job1(1 + k)
                        w = wq if k < 2 else wk
                        for a in range(2):
                            ins = pe.matmul(W1[:, a * TB:(a + 1) * TB], w[:, 2 * (k % 2) + a, :], hT[:],
                                            start=True, stop=True)
                        ins.then_inc(w1_full, 1)
                    if what == "vT" and pre:
                        job1(5)
                        pe.matmul(W1[:, 0:TB], wv[:], hT[:], start=True, stop=True).then_inc(w1_full, 1)
                    if what == "windows" and pre:
                        job1(6)
                        for w in range(4):
                            ins = pe.transpose(W1[:, w * P:(w + 1) * P], vT[:, w * BK:w * BK + P], ident[:])
                        ins.then_inc(w1_full, 1)
                    if what == "scores" and main:
                        pe.wait_ge(qk_done, main.n * 4 + 4)
                        for g in range(4):
                            u = 4 * k + g
                            if not (main.first and u < 2):
                                pe.wait_ge(s_free, main.n * 8 + u - 1)
                            r = slice(32 * g, 32 * g + 32)
                            for v in range(2):
                                w = 2 * k + v
                                for a in range(4):
                                    ins = pe.matmul(S[BK * v:BK * v + BK, u % 2, a * P:(a + 1) * P],
                                                    qs[main.p][r, a, w * BK:(w + 1) * BK],
                                                    ks[main.p][r, a, w * BK:w * BK + P],
                                                    start=(a == 0), stop=False, skip_group_check=True)
                            ins = pe.matmul(S[:, u % 2, :], identb[:], causal[:], start=False, stop=True,
                                            skip_group_check=True)
                            ins.then_inc(s_full, 1)
                    if what == "shift" and main:
                        pe.wait_ge(mpad_done, main.n * 2 + k + 1)
                        if not (main.first and k == 0):
                            pe.wait_ge(mi_free, main.n * 4 + k)
                        for a in range(4):
                            ins = pe.transpose(MT[:, a, :], mpad[:, k, a].rearrange("p g r -> p (g r)"),
                                               ident16[:])
                        ins.then_inc(mi_full, 1)
                    if what == "weights" and main:
                        t, g = k // 4, k % 4
                        pe.wait_ge(mi_free, main.n * 4 + t + 1)
                        if not (main.first and k < 2):
                            pe.wait_ge(exp_done, main.n * 8 + k - 1)
                        r = slice(32 * g, 32 * g + 32)
                        for v in range(2):
                            for a in range(4):
                                ins = pe.matmul(ST[:, k % 2, (4 * v + a) * BK:(4 * v + a + 1) * BK],
                                                ks[main.p][r, a, (2 * t + v) * BK:(2 * t + v) * BK + P],
                                                q2[r, t, a, v * BK:(v + 1) * BK], start=True, stop=True)
                        ins.then_inc(st_full, 1)
                    if what == "values" and main:
                        t, g = k // 4, k % 4
                        if g == 0 and not (main.first and t == 0):
                            pe.wait_ge(ot_free, main.n * 2 + t)
                        if k == 0:
                            pe.wait_ge(w1_free, main.n * 7 + 7)
                        pe.wait_ge(causal_done, main.n * 8 + k + 1)
                        for v in range(2):
                            for a in range(4):
                                ins = pe.matmul(OT[32 * g:32 * g + 32, a * P + v * BK:a * P + (v + 1) * BK],
                                                va[main.p][:, 2 * t + v, 4 * a + g, :],
                                                pt[:, k % 4, (4 * v + a) * BK:(4 * v + a + 1) * BK],
                                                start=True, stop=True)
                        ins.then_inc(pv_done, 1)
                    if what == "back" and main:
                        pe.wait_ge(ot_free, main.n * 2 + k + 1)
                        pe.wait_ge(mi_free, main.n * 4 + 2 + k)
                        for a in range(4):
                            ins = pe.transpose(MI[:, a * P:(a + 1) * P], ots[:, k, a * P:(a + 1) * P], ident[:])
                        ins.then_inc(mi_full, 1)
                    if what == "output" and post:
                        if not post.first:
                            pe.wait_ge(w3_free, post.n)
                            pe.wait_ge(x1_done, post.n)
                        pe.wait_ge(mi_free, post.n * 4 + 4)
                        for a in range(2):
                            ins = pe.transpose(W3[:, a * P:(a + 1) * P], ob[post.p][:, a, :], ident[:])
                        ins.then_inc(w3_full, 1)
                        pe.wait_ge(w3_free, post.n + 1)
                        for a in range(2):
                            ins = pe.matmul(W3[:, a * P:(a + 1) * P], aT[:, a * P:(a + 1) * P], wo[:],
                                            start=True, stop=True)
                        ins.then_inc(w3_full, 1)

            skewed(pe, NB, step)


def split_weights(nc, tag, keep, w1, w2):
    with ExitStack() as ctx:
        m = Mem(nc, ctx, tag)
        parts = []
        n = w1.shape[1]
        size = min(n, 2048)
        stage = m.sb("stage", [P, 2, size])
        landed = [m.sem("landed0"), m.sem("landed1")]
        high_done, low_done = m.sem("high_done"), m.sem("low_done")
        for src, high, low in ((w1, keep["w1h"], keep["w1l"]), (w2, keep["w2h"], keep["w2l"])):
            for c in range(n // size):
                s = slice(c * size, (c + 1) * size)
                parts.append((src[:, s], high[:, s], low[:, s]))
        block = ctx.enter_context(nc.Block())

        @block.sync
        def _(sp):
            for c, (src, _, _) in enumerate(parts):
                wait(sp, low_done, c - 1)
                sp.dma_start(stage[:, c % 2], src).then_inc(landed[c % 2], 16)

        @block.scalar
        def _(act):
            for c, (_, high, _) in enumerate(parts):
                act.wait_ge(landed[c % 2], 16 * (c // 2 + 1))
                act.activation(high, stage[:, c % 2], ACT.Copy).then_inc(high_done, 1)

        @block.vector
        def _(dve):
            for c, (_, high, low) in enumerate(parts):
                dve.wait_ge(high_done, c + 1)
                dve.tensor_tensor(low, stage[:, c % 2], high.bitcast(F32), ALU.subtract).then_inc(low_done, 1)


def experts(nc, tag, keep, d, n_exp, gelu, norm_first=False, transposed=False, gates=None, out=None):
    with ExitStack() as ctx:
        m = Mem(nc, ctx, tag)
        E_ = n_exp
        b1 = m.sb("b1", [P, E_ * FB])
        cols = m.sb("cols", [P, 4])
        b2 = m.sb("b2", [E_, C])
        hf = m.sb("hf", [P, 2, FB, CT])
        hh = m.sb("hh", [P, 2, FB, CT], F32R)
        hl = m.sb("hl", [P, 2, FB, CT], F32R)
        acc = m.sb("acc", [P, 2, CT])
        half = m.sb("half", [P, 8])
        st = m.sb("st", [P, 4, 6])
        mv = m.sb("mv", [P, 4, 2])
        rstd = m.sb("rstd", [P, 4])
        r = m.sb("r", [P, 4, C])
        xn = m.sb("xn", [P, 4, C]) if norm_first else r
        if transposed:
            xT = m.sb("xT", [P, CT])
        if norm_first:
            st0 = m.sb("st0", [P, 4, 6])
            mv0 = m.sb("mv0", [P, 4, 2])
            rstd0 = m.sb("rstd0", [P, 4])
            hn = m.sb("hn", [P, 4, C])
            h2 = m.sb("h2", [P, CT])
        else:
            tmp = m.sb("tmp", [P, CT])
            G = [m.sb(f"G{p}", [P, E_, CT]) for p in range(2)]
            g8 = [m.sb(f"g8{p}", [E_, CT]) for p in range(2)]
        HB = m.ps("HB", [P, 4, CT])
        YB = m.ps("YB", [P, 2, CT])
        PB = m.ps("PB", [P, CT])
        QB = m.ps("QB", [P, CT])

        loaded, half_set = m.sem("loaded"), m.sem("half_set")
        g_in = [m.sem(f"g_in{p}") for p in range(2)]
        ln0 = m.sem("ln0")
        var0_done, rstd0_done, pool0 = m.sem("var0_done"), m.sem("rstd0_done"), m.sem("pool0")
        hn_done = m.sem("hn_done")
        qb_full, qb_free = m.sem("qb_full"), m.sem("qb_free")
        xh_done, xl_done = m.sem("xh_done"), m.sem("xl_done")
        h_full, h_free = m.sem("h_full"), m.sem("h_free")
        hi_done, lo_done = m.sem("hi_done"), m.sem("lo_done")
        y_full, y_free = m.sem("y_full"), m.sem("y_free")
        comb = m.sem("comb")
        acc_done = m.sem("acc_done")
        pb_full, pb_free = m.sem("pb_full"), m.sem("pb_free")
        ln1 = m.sem("ln1")
        var_done, rstd_done, pool1 = m.sem("var_done"), m.sem("rstd_done"), m.sem("pool1")
        passed_pool, passed_dve = m.sem("passed_pool"), m.sem("passed_dve")
        xn_done, xa_done = m.sem("xn_done"), m.sem("xa_done")
        xT_done, xTh_done, xTl_done = m.sem("xT_done"), m.sem("xTh_done"), m.sem("xTl_done")
        stored = m.sem("stored")
        jobs = 3 if transposed else 1
        loads = [(b1[:], d["b1"]), (cols[:], d["cols"]), (b2[:], d["b2"])]

        def par(turn, e):
            return turn.p if E_ % 2 else e % 2

        order = [("pre", 0)]
        for e in range(E_):
            order += [("hidden", e + 1), ("down", e)]
            if e == min(0, E_ - 1):
                order += [("post", 0)]
            if e == min(1, E_ - 1):
                order += [("post", 1)]
            if e == min(2, E_ - 1):
                order += [("post", 2)]

        def chunk(t, turn):
            return t[:, ds(turn.n * CT, CT)]

        def parts_of(step):
            def go(pre, main, post):
                for what, k in order:
                    if what == "pre" and pre:
                        step("pre", pre, 0)
                    if what == "hidden":
                        if k < E_ and main:
                            step("hidden", main, k)
                        if k == E_ and pre:
                            step("hidden", pre, 0)
                    if what == "down" and main:
                        step("down", main, k)
                    if what == "post" and post:
                        if k == 0 or transposed:
                            step("post%d" % k, post, 0)
            return go

        block = ctx.enter_context(nc.Block())

        @block.sync
        def _(sp):
            for dst, src in loads:
                sp.dma_start(dst, src).then_inc(loaded, 16)

            def step(what, t, k):
                if what == "pre" and gates is not None:
                    if not t.early:
                        sp.wait_ge(acc_done, t.n - 1)
                    src = gates[:, ds(t.n * CT, CT)]
                    sp.dma_start(g8[t.p][:], src).then_inc(g_in[t.p], 16)
                    sp.dma_start(G[t.p][:], src[None, :, :].to_broadcast([P, E_, CT])).then_inc(g_in[t.p], 16)
                if what == "post0" and out is not None:
                    sp.wait_ge(xn_done, t.n + 1)
                    sp.dma_start(out[:, ds(t.n * 4, 4), :], xn[:]).then_inc(stored, 16)

            skewed(sp, NC_, parts_of(step))
            if out is not None:
                sp.wait_ge(stored, 16 * NC_)

        @block.gpsimd
        def _(pool):
            pool.memset(half[:], -0.5).then_inc(half_set, 1)
            pool.wait_ge(half_set, 1)

            def step(what, t, k):
                if what == "pre" and norm_first:
                    pool.wait_ge(var0_done, t.n + 1)
                    settle(pool, passed_pool)
                    c = Tally(pool, pool0, 1, t.n)
                    c.link(pool.tensor_scalar(rstd0[:], mv0[:, :, 1], EPS, 1.0, ALU.add, ALU.mult))
                    pool.tensor_tensor(rstd0[:], rstd0[:], half[:, 0:4], ALU.pow).then_inc(rstd0_done, 1)
                if what == "post0":
                    pool.wait_ge(var_done, t.n + 1)
                    settle(pool, passed_pool)
                    c = Tally(pool, pool1, 1, t.n)
                    c.link(pool.tensor_scalar(rstd[:], mv[:, :, 1], EPS, 1.0, ALU.add, ALU.mult))
                    pool.tensor_tensor(rstd[:], rstd[:], half[:, 0:4], ALU.pow).then_inc(rstd_done, 1)
                    if out is None:
                        pool.wait_ge(xn_done, t.n + 1)
                        settle(pool, passed_pool)
                        pool.tensor_copy(keep["xa"][:, ds(t.n * 4, 4), :], xn[:]).then_inc(xa_done, 1)

            skewed(pool, NC_, parts_of(step))

        @block.scalar
        def _(act):
            act.wait_ge(loaded, 16 * len(loads))

            def step(what, t, k):
                if what == "pre" and norm_first:
                    act.wait_ge(qb_full, t.n + 1)
                    if not t.first:
                        act.wait_ge(xl_done, t.n)
                    act.activation(h2[:], QB[:], ACT.Identity, scale=cols[:, 0:1],
                                   bias=cols[:, 1:2]).then_inc(qb_free, 1)
                    act.wait_ge(qb_free, t.n + 1)
                    act.activation(chunk(keep["xh"], t), h2[:], ACT.Copy).then_inc(xh_done, 1)
                if what == "hidden":
                    j, q = t.n * E_ + k, par(t, k)
                    new = isinstance(j, int) and j < 2
                    for f in range(FB):
                        act.wait_ge(h_full, j * 4 + f + 1)
                        if f == 0 and not new:
                            act.wait_ge(lo_done, j * 2 - 2)
                        act.activation(hf[:, q, f], HB[:, f], gelu,
                                       bias=b1[:, k * FB + f:k * FB + f + 1]).then_inc(h_free, 1)
                        if f % 2:
                            act.wait_ge(h_free, j * 4 + f + 1)
                            if f == 1 and not new:
                                act.wait_ge(y_full, j - 1)
                            act.activation(hh[:, q, f - 1:f + 1], hf[:, q, f - 1:f + 1],
                                           ACT.Copy).then_inc(hi_done, 1)
                if what == "post1":
                    act.wait_ge(pb_full, t.n * jobs + 2)
                    if not t.first:
                        act.wait_ge(xTl_done, t.n)
                        act.wait_ge(pb_full, t.n * jobs)
                    act.activation(xT[:], PB[:], ACT.Copy).then_inc(pb_free, 1)
                    act.wait_ge(pb_free, t.n * jobs + 2)
                    act.activation(chunk(keep["xh"], t), xT[:], ACT.Copy).then_inc(xTh_done, 1)

            skewed(act, NC_, parts_of(step))

        @block.vector
        def _(dve):
            dve.wait_ge(loaded, 16 * len(loads))

            def step(what, t, k):
                if what == "pre" and norm_first:
                    c = Tally(dve, ln0, 11, t.n)
                    x1 = lambda a: keep["x1"][:, ds(t.n * 4 + a, 1), :].rearrange("p a c -> p (a c)")
                    for a in range(4):
                        c.inc(dve.bn_stats(st0[:, a, :], x1(a)))
                    c.wait()
                    settle(dve, passed_dve)
                    for a in range(4):
                        ins = dve.bn_aggr(mv0[:, a, :], st0[:, a, :])
                        ins.then_inc(var0_done, 1) if a == 3 else c.inc(ins)
                    if not t.first:
                        dve.wait_ge(qb_full, t.n)
                    dve.wait_ge(rstd0_done, t.n + 1)
                    c.n = 7
                    for a in range(4):
                        c.inc(dve.tensor_scalar(hn[:, a, :], x1(a), mv0[:, a, 0:1], rstd0[:, a:a + 1],
                                                ALU.subtract, ALU.mult))
                    dve.wait_ge(xh_done, t.n + 1)
                    dve.tensor_tensor(chunk(keep["xl"], t), h2[:], chunk(keep["xh"], t).bitcast(F32),
                                      ALU.subtract).then_inc(xl_done, 1)
                if what == "hidden":
                    j, q = t.n * E_ + k, par(t, k)
                    for f in (0, 2):
                        dve.wait_ge(hi_done, j * 2 + f // 2 + 1)
                        if f == 0 and not (isinstance(j, int) and j < 2):
                            dve.wait_ge(y_full, j - 1)
                        dve.tensor_tensor(hl[:, q, f:f + 2], hf[:, q, f:f + 2], hh[:, q, f:f + 2].bitcast(F32),
                                          ALU.subtract).then_inc(lo_done, 1)
                if what == "down":
                    j, q = t.n * E_ + k, par(t, k)
                    dve.wait_ge(y_full, j + 1)
                    if k == 0 and not t.early:
                        dve.wait_ge(pb_full, (t.n - 1) * jobs)
                    if norm_first:
                        dve.tensor_scalar(acc[:, t.p], YB[:, q], cols[:, 2:3], None,
                                          ALU.add).then_inc(y_free, 1)
                    else:
                        c = Tally(dve, comb, E_ - 2, t.n)
                        c.n = k - 1
                        if k == 0:
                            dve.wait_ge(g_in[t.p], (t.half + 1) * 32)
                            dve.tensor_tensor(acc[:, t.p], YB[:, q], G[t.p][:, k], ALU.mult).then_inc(y_free, 1)
                            dve.wait_ge(y_free, j + 1)
                            dve.wait_ge(qb_full, t.n + 1)
                            dve.tensor_tensor(acc[:, t.p], acc[:, t.p], QB[:], ALU.add).then_inc(qb_free, 1)
                            dve.wait_ge(qb_free, t.n + 1)
                        else:
                            dve.tensor_tensor(tmp[:], YB[:, q], G[t.p][:, k], ALU.mult).then_inc(y_free, 1)
                            dve.wait_ge(y_free, j + 1)
                            ins = dve.tensor_tensor(acc[:, t.p], acc[:, t.p], tmp[:], ALU.add)
                            if k < E_ - 1:
                                c.link(ins)
                            else:
                                ins.then_inc(acc_done, 1)
                if what == "post0":
                    dve.wait_ge(pb_full, t.n * jobs + 1)
                    res = keep["xs" if norm_first else "xa"]
                    if not t.first:
                        if out is None:
                            dve.wait_ge(xa_done, t.n)
                        else:
                            dve.wait_ge(stored, t.n * 16)
                    dve.tensor_tensor(r[:], PB[:].rearrange("p (a c) -> p a c", a=4),
                                      res[:, ds(t.n * 4, 4), :], ALU.add).then_inc(pb_free, 1)
                    dve.wait_ge(pb_free, t.n * jobs + 1)
                    c = Tally(dve, ln1, 10, t.n)
                    for a in range(4):
                        c.inc(dve.bn_stats(st[:, a, :], r[:, a, :]))
                    c.wait()
                    settle(dve, passed_dve)
                    for a in range(4):
                        ins = dve.bn_aggr(mv[:, a, :], st[:, a, :])
                        ins.then_inc(var_done, 1) if a == 3 else c.inc(ins)
                    if transposed and not t.first:
                        dve.wait_ge(pb_full, t.n * jobs)
                    dve.wait_ge(rstd_done, t.n + 1)
                    for a in range(4):
                        ins = dve.tensor_scalar(xn[:, a, :], r[:, a, :], mv[:, a, 0:1], rstd[:, a:a + 1],
                                                ALU.subtract, ALU.mult)
                        ins.then_inc(xn_done, 1) if a == 3 else c.inc(ins)
                if what == "post1":
                    dve.wait_ge(xTh_done, t.n + 1)
                    dve.tensor_tensor(chunk(keep["xl"], t), xT[:], chunk(keep["xh"], t).bitcast(F32),
                                      ALU.subtract).then_inc(xTl_done, 1)
                if what == "post2":
                    dve.wait_ge(pb_full, t.n * jobs + 3)
                    dve.tensor_copy(keep["logits"][:, ds(t.n * 4, 4), :],
                                    PB[:, 0:4 * E].rearrange("p (a e) -> p a e", a=4)).then_inc(pb_free, 1)

            skewed(dve, NC_, parts_of(step))

        @block.tensor
        def _(pe):
            pe.wait_ge(loaded, 16 * len(loads))

            def split_product(dst, wh, wl, xh, xl, first, last):
                pe.matmul(dst, wh, xh, start=first, stop=False)
                pe.matmul(dst, wh, xl, start=False, stop=False)
                return pe.matmul(dst, wl, xh, start=False, stop=last)

            def step(what, t, k):
                if what == "pre" and norm_first:
                    pe.wait_ge(ln0, (t.n + 1) * 11)
                    if not t.first:
                        pe.wait_ge(qb_free, t.n)
                    for a in range(4):
                        ins = pe.transpose(QB[:, a * P:(a + 1) * P], hn[:, a, :], keep["ident"][:])
                    ins.then_inc(qb_full, 1)
                if what == "hidden":
                    j = t.n * E_ + k
                    if k == 0 and norm_first:
                        pe.wait_ge(xh_done, t.n + 1)
                        pe.wait_ge(xl_done, t.n + 1)
                    for f in range(FB):
                        if not (isinstance(j, int) and j < 1):
                            pe.wait_ge(h_free, j * 4 + f - 3)
                        s = slice((k * FB + f) * P, (k * FB + f + 1) * P)
                        split_product(HB[:, f], keep["w1h"][:, s], keep["w1l"][:, s], chunk(keep["xh"], t),
                                      chunk(keep["xl"], t), True, True).then_inc(h_full, 1)
                if what == "down":
                    j, q = t.n * E_ + k, par(t, k)
                    if not (isinstance(j, int) and j < 2):
                        pe.wait_ge(y_free, j - 1)
                    for f in range(FB):
                        if f % 2 == 0:
                            pe.wait_ge(lo_done, j * 2 + f // 2 + 1)
                        s = slice((k * FB + f) * P, (k * FB + f + 1) * P)
                        ins = split_product(YB[:, q], keep["w2h"][:, s], keep["w2l"][:, s], hh[:, q, f],
                                            hl[:, q, f], f == 0, f == FB - 1)
                    ins.then_inc(y_full, 1)
                    if k == 0 and not norm_first:
                        pe.wait_ge(g_in[t.p], (t.half + 1) * 32)
                        if not t.first:
                            pe.wait_ge(qb_free, t.n)
                        pe.matmul(QB[:], b2[:], g8[t.p][:], start=True, stop=True).then_inc(qb_full, 1)
                if what == "post0":
                    if norm_first:
                        pe.wait_ge(y_free, t.n + 1)
                    else:
                        pe.wait_ge(acc_done, t.n + 1)
                    if not t.first:
                        pe.wait_ge(pb_free, t.n * jobs)
                    for a in range(4):
                        ins = pe.transpose(PB[:, a * P:(a + 1) * P], acc[:, t.p, a * P:(a + 1) * P],
                                           keep["ident"][:])
                    ins.then_inc(pb_full, 1)
                if what == "post1":
                    pe.wait_ge(xn_done, t.n + 1)
                    pe.wait_ge(pb_free, t.n * jobs + 1)
                    for a in range(4):
                        ins = pe.transpose(PB[:, a * P:(a + 1) * P], xn[:, a, :], keep["ident"][:])
                    ins.then_inc(pb_full, 1)
                if what == "post2":
                    pe.wait_ge(pb_free, t.n * jobs + 2)
                    for a in range(4):
                        ins = pe.matmul(PB[:, a * E:(a + 1) * E], xT[:, a * P:(a + 1) * P],
                                        keep["gate0"][:], start=True, stop=True)
                    ins.then_inc(pb_full, 1)

            skewed(pe, NC_, parts_of(step))


def threshold(nc, keep, gates_dram):
    with ExitStack() as ctx:
        m = Mem(nc, ctx, "t")
        N = NT * E
        L = keep["logits"][:].rearrange("p a e -> p (a e)")
        Ls = m.sb("Ls", [P, N])
        below = m.sb("below", [P, N])
        ones = m.sb("ones", [P, P])
        cnt = m.sb("cnt", [P, 1])
        neg = m.sb("neg", [P, 1])
        sign = m.sb("sign", [P, 1])
        rank = m.sb("rank", [P, 1])
        bit = m.sb("bit", [P, 1])
        bit_u = m.sb("bit_u", [P, 1], U32)
        found = m.sb("found", [P, 1], U32)
        cand = m.sb("cand", [P, 1], U32)
        add = m.sb("add", [P, 1], U32)
        kth = m.sb("kth", [P, 1])
        gt = m.sb("gt", [P, N])
        gT = m.sb("gT", [P, 2, P])
        CP = m.ps("CP", [P, 512])
        TP = m.ps("TP", [P, 512])
        own = m.sem("own")
        counted, summed = m.sem("counted"), m.sem("summed")
        turned, copied, sent = m.sem("turned"), m.sem("copied"), m.sem("sent")
        block = ctx.enter_context(nc.Block())
        BITS = 31

        @block.vector
        def _(dve):
            t = Tally(dve, own, 0, 0)
            dve.memset(ones[:], 1.0)
            dve.memset(bit[:], float(2 ** (BITS - 1)))
            t.link(dve.memset(found[:], 0))
            dve.tensor_scalar(below[:], L, 0.0, None, ALU.is_lt, ALU.add, accum_out=cnt[:]).then_inc(counted, 1)
            dve.wait_ge(summed, 1)
            t.link(dve.tensor_scalar(neg[:], CP[:, 0:1], float(KEEP_FROM), None, ALU.is_ge))
            t.link(dve.tensor_scalar(sign[:], neg[:], -2.0, 1.0, ALU.mult, ALU.add))
            t.link(dve.tensor_scalar(rank[:], neg[:], float(T * E - 2 * KEEP_FROM + 1), float(KEEP_FROM - 1),
                                     ALU.mult, ALU.add))
            t.link(dve.tensor_scalar(Ls[:], L, sign[:], None, ALU.mult))
            first = t.n
            with dve.Fori(0, BITS) as i:
                t = Tally(dve, own, 5, i)
                t.n = first
                t.link(dve.tensor_copy(bit_u[:], bit[:]))
                t.link(dve.tensor_tensor(cand[:], found[:], bit_u[:], ALU.bitwise_or))
                dve.tensor_scalar(below[:], Ls[:], cand[:].bitcast(F32), None, ALU.is_lt, ALU.add,
                                  accum_out=cnt[:]).then_inc(counted, 1)
                dve.wait_ge(summed, i + 2)
                t.link(dve.tensor_scalar(add[:], CP[:, 0:1], rank[:], bit[:], ALU.is_le, ALU.mult))
                t.link(dve.tensor_tensor(found[:], found[:], add[:], ALU.bitwise_or))
                t.link(dve.tensor_scalar(bit[:], bit[:], 0.5, None, ALU.mult))
            t = Tally(dve, own, 0, 0)
            t.n = first + 5 * BITS
            t.link(dve.tensor_tensor(kth[:], found[:].bitcast(F32), sign[:], ALU.mult))
            dve.scalar_tensor_tensor(out=gt[:], in0=L, scalar=kth[:], in1=L, op0=ALU.is_ge,
                                     op1=ALU.mult).then_inc(counted, 1)
            dve.wait_ge(turned, 1)
            dve.tensor_copy(gT[:].rearrange("p a b -> p (a b)"), TP[:, 0:N]).then_inc(copied, 1)

        @block.tensor
        def _(pe):
            pe.wait_ge(counted, 1)
            pe.matmul(CP[:, 0:1], ones[:], cnt[:], start=True, stop=True).then_inc(summed, 1)
            with pe.Fori(0, BITS) as i:
                pe.wait_ge(counted, i + 2)
                pe.matmul(CP[:, 0:1], ones[:], cnt[:], start=True, stop=True).then_inc(summed, 1)
            pe.wait_ge(counted, BITS + 2)
            for a in range(2):
                ins = pe.transpose(TP[:, a * P:(a + 1) * P], gt[:, a * P:(a + 1) * P], keep["ident"][:])
            ins.then_inc(turned, 1)

        @block.sync
        def _(sp):
            sp.wait_ge(copied, 1)
            for a in range(2):
                for t_ in range(16):
                    sp.dma_start(gates_dram[:, (a * 16 + t_) * P:(a * 16 + t_ + 1) * P],
                                 gT[t_ * E:(t_ + 1) * E, a, :]).then_inc(sent, 16)
            sp.wait_ge(sent, 16 * 32)


ORDER_1 = [("scores", 0), ("mix", 0), ("copy", 0), ("scores", 1), ("shift", 0), ("xT", 0), ("context", 0),
           ("weights", 0), ("shift", 1), ("project", 0), ("values", 0), ("weights", 1), ("next", 0),
           ("linear", 0), ("values", 1), ("back", 0), ("router", 0), ("features", 0), ("back", 1),
           ("gates", 0), ("qT", 0)]
LH, GH = 4, 12
GW = GH * HD


def attention_1(nc, d, keep, gates):
    with ExitStack() as ctx:
        m = Mem(nc, ctx, "b")
        wql = m.sb("wql", [P, P])
        wkl = m.sb("wkl", [P, P])
        wg = m.sb("wg", [P, 2 * GW + C])
        wo = m.sb("wo", [P, P])
        cols = m.sb("cols", [P, 4])
        bo = m.sb("bo", [P, P])
        ident16 = m.sb("ident16", [P, P], F16)
        identb = m.sb("identb", [P, P], BF16)
        causal = m.sb("causal", [P, 2, P], BF16)
        causalT = m.sb("causalT", [P, 2, P], BF16)
        same_head = m.sb("same_head", [GW, GW])
        before = m.sb("before", [P, E, E])
        gate1 = m.sb("gate1", [P, E])
        xs = [m.sb(f"xs{p}", [P, 2, C]) for p in range(2)]
        xb = [m.sb(f"xb{p}", [P, 2, C]) for p in range(2)]
        xT = m.sb("xT", [P, TB])
        full = m.sb("full", [P, 2, TB])
        high = m.sb("high", [P, 2, TB], F16)
        qs = [m.sb(f"qs{p}", [P, TB], F16) for p in range(2)]
        ks = [m.sb(f"ks{p}", [P, TB], F16) for p in range(2)]
        va = [m.sb(f"va{p}", [P, 2, LH, 32]) for p in range(2)]
        gv = [m.sb(f"gv{p}", [P, 2, GW + 1]) for p in range(2)]
        kf = [m.sb(f"kf{p}", [P, 2, GW]) for p in range(2)]
        qT = [m.sb(f"qT{p}", [GW, TB]) for p in range(2)]
        qm = m.sb("qm", [P, 2, GH])
        qd = m.sb("qd", [P, 2, GW])
        qe = m.sb("qe", [P, 2, GW])
        qsum = m.sb("qsum", [P, 2, GH])
        qr = m.sb("qr", [P, 2, GH])
        qn = m.sb("qn", [P, 2, GW])
        kn = m.sb("kn", [P, 2, GW])
        ke = m.sb("ke", [P, 2, GW])
        mx = m.sb("mx", [P, 2, LH])
        mpad = m.sb("mpad", [P, 2, LH, 32], F16)
        q2 = m.sb("q2", [P, 2, P], F16)
        pt = m.sb("pt", [P, 2, LH, 2 * P])
        ots = m.sb("ots", [P, 2, P])
        rc = m.sb("rc", [P, 2, LH])
        den = m.sb("den", [GW, 3])
        rinv = m.sb("rinv", [GW, 3])
        ctxn = m.sb("ctxn", [GW, 3, GW])
        ob = [m.sb(f"ob{p}", [P, 2, C]) for p in range(2)]
        aT = m.sb("aT", [P, TB])
        half = m.sb("half", [P, 2])
        r = m.sb("r", [P, 2, C])
        st = m.sb("st", [P, 2, 6])
        mv = m.sb("mv", [P, 2, 2])
        rstd = m.sb("rstd", [P, 2])
        xn = m.sb("xn", [P, 2, C])
        x3T = m.sb("x3T", [P, TB])
        lg = m.sb("lg", [P, 2, E])
        lm = m.sb("lm", [P, 2])
        ld = m.sb("ld", [P, 2, E])
        le = m.sb("le", [P, 2, E])
        gtr = m.sb("gtr", [P, 2, E, E])
        eqr = m.sb("eqr", [P, 2, E, E])
        rank = m.sb("rank", [P, 2, E])
        sel = m.sb("sel", [P, 2, E])
        gsum = m.sb("gsum", [P, 2])
        grec = m.sb("grec", [P, 2])
        gt = m.sb("gt", [P, 2, E])
        gT = m.sb("gT", [2 * E, P])

        SS = m.ps("SS", [P, 2, 512])
        OT = m.ps("OT", [P, 512])
        MI = m.ps("MI", [P, 512])
        W1 = m.ps("W1", [P, 512])
        WG = m.ps("WG", [P, 2, 512])
        W3 = m.ps("W3", [P, 512])
        MT = MI[:, 0:P // 2].bitcast(F16)

        names = ("loaded cleared copied xb_done w1_full w1_free high_done qk_done wg_full wg_free "
                 "feat_own first_heads kn_done ke_done qd_done qe_done qn_done ss_full ss_free mx_own mpad_done "
                 "mi_full mi_free pv_done ot_free norm_own ctx_own o_done w3_full w3_free r_own var_done "
                 "pool_ln rstd_done xn_done xa_done xh_done xl_done lg_own ld_done le_done gt_done sent "
                 "passed_pool passed_dve")
        s = {n: m.sem(n) for n in names.split()}
        loads = [(wql[:], "b_wql"), (wkl[:], "b_wkl"), (wg[:], "b_wg"), (wo[:], "b_wo"), (cols[:], "b_cols"),
                 (ident16[:], "ident16"), (identb[:], "identb"), (causal[:], "causal128"),
                 (causalT[:], "causal128T"), (same_head[:], "same_head"), (before[:], "before"),
                 (gate1[:], "gate1")]
        scale = float(HD) ** -0.5

        def ready(eng):
            eng.wait_ge(s["loaded"], 16 * (len(loads) + 1))
            eng.wait_ge(s["cleared"], 3)

        def parts_of(act):
            def go(pre, main, post):
                for what, k in ORDER_1:
                    t = {"copy": pre, "xT": pre, "project": pre, "features": pre, "qT": pre, "mix": post,
                         "next": post, "router": post, "gates": post}.get(what, main)
                    if t:
                        act(what, t, k)
            return go

        block = ctx.enter_context(nc.Block())

        @block.sync
        def _(sp):
            for dst, name in loads:
                sp.dma_start(dst, d[name]).then_inc(s["loaded"], 16)
            sp.dma_start(bo[:], d["b_bo"].to_broadcast([P, C])).then_inc(s["loaded"], 16)

            def part(what, t, k):
                if what == "gates":
                    sp.wait_ge(s["w3_free"], t.n * 5 + 5)
                    for a in range(2):
                        sp.dma_start(gates[:, ds(t.n * TB + a * P, P)],
                                     gT[a * E:(a + 1) * E, :]).then_inc(s["sent"], 16)

            skewed(sp, NB, parts_of(part))
            sp.wait_ge(s["sent"], 32 * NB)

        @block.gpsimd
        def _(pool):
            pool.memset(half[:], -0.5)
            for v in va:
                pool.memset(v[:], 0.0)
            for v in ob:
                pool.memset(v[:], 0.0)
            pool.memset(mpad[:], 0.0).then_inc(s["cleared"], 1)
            pool.wait_ge(s["cleared"], 1)
            for a in range(2):
                pool.memset(va[a][:, :, :, HD:HD + 1], 1.0)
                pool.memset(gv[a][:, :, GW:GW + 1], 1.0).then_inc(s["cleared"], 1)
            ready(pool)

            def part(what, t, k):
                if what == "copy":
                    if not t.early:
                        pool.wait_ge(s["w1_full"], (t.n - 2) * 3 + 1)
                        pool.wait_ge(s["xn_done"], t.n - 1)
                    settle(pool, s["passed_pool"])
                    pool.tensor_copy(xs[t.p][:], keep["xa"][:, ds(t.n * 2, 2), :]).then_inc(s["copied"], 1)
                    pool.wait_ge(s["copied"], t.n + 1)
                    for a in range(2):
                        ins = pool.tensor_tensor(xb[t.p][:, a, :], xs[t.p][:, a, :], bo[:], ALU.add)
                    ins.then_inc(s["xb_done"], 1)
                if what == "project":
                    pool.wait_ge(s["w1_free"], t.n * 3 + 2)
                    settle(pool, s["passed_pool"])
                    pool.tensor_copy(high[:], full[:]).then_inc(s["high_done"], 1)
                if what == "mix":
                    pool.wait_ge(s["var_done"], t.n + 1)
                    settle(pool, s["passed_pool"])
                    c = Tally(pool, s["pool_ln"], 1, t.n)
                    c.link(pool.tensor_scalar(rstd[:], mv[:, :, 1], EPS, 1.0, ALU.add, ALU.mult))
                    pool.tensor_tensor(rstd[:], rstd[:], half[:], ALU.pow).then_inc(s["rstd_done"], 1)
                    pool.wait_ge(s["xn_done"], t.n + 1)
                    settle(pool, s["passed_pool"])
                    pool.tensor_copy(keep["xa"][:, ds(t.n * 2, 2), :], xn[:]).then_inc(s["xa_done"], 1)

            skewed(pool, NB, parts_of(part))

        @block.scalar
        def _(act):
            ready(act)

            def part(what, t, k):
                if what == "xT":
                    act.wait_ge(s["w1_full"], t.n * 3 + 1)
                    if not t.first:
                        act.wait_ge(s["wg_full"], t.n)
                    act.activation(xT[:], W1[:, 0:TB], ACT.Copy).then_inc(s["w1_free"], 1)
                if what == "project":
                    act.wait_ge(s["w1_full"], t.n * 3 + 2)
                    if not t.first:
                        act.wait_ge(s["qk_done"], t.n)
                    act.activation(full[:, 0], W1[:, 0:TB], ACT.Copy)
                    act.activation(full[:, 1], W1[:, TB:2 * TB], ACT.Identity,
                                   bias=cols[:, 0:1]).then_inc(s["w1_free"], 1)
                if what == "features":
                    act.wait_ge(s["kn_done"], t.n + 1)
                    if not t.first:
                        act.wait_ge(s["wg_free"], t.n)
                    act.activation(ke[:], kn[:], ACT.Exp).then_inc(s["ke_done"], 1)
                    act.wait_ge(s["qd_done"], t.n + 1)
                    act.activation(qe[:], qd[:], ACT.Exp).then_inc(s["qe_done"], 1)
                if what == "qT":
                    act.wait_ge(s["w1_full"], t.n * 3 + 3)
                    if not t.early:
                        act.wait_ge(s["mi_full"], (t.n - 2) * 6 + 4)
                    act.activation(qT[t.p][:], W1[0:GW, 0:TB], ACT.Copy).then_inc(s["w1_free"], 1)
                if what == "weights":
                    act.wait_ge(s["ss_full"], t.n * 4 + 3 + k)
                    if not t.first:
                        act.wait_ge(s["pv_done"], t.n * 2 - 1 + k)
                    n = P * (k + 1)
                    act.activation(pt[:, k, :, 0:n],
                                   SS[:].rearrange("p b (h j) -> p (b h) j", h=2)[:, :, 0:n],
                                   ACT.Exp, scale=scale).then_inc(s["ss_free"], 1)
                if what == "back":
                    act.wait_ge(s["pv_done"], t.n * 2 + k + 1)
                    if not t.first:
                        act.wait_ge(s["mi_full"], t.n * 6 - 1 + k)
                    act.activation(ots[:, k], OT[:, k * P:(k + 1) * P], ACT.Copy).then_inc(s["ot_free"], 1)
                if what == "mix":
                    act.wait_ge(s["w3_full"], t.n * 5 + 1)
                    act.activation(aT[:], W3[:, 0:TB], ACT.Copy).then_inc(s["w3_free"], 1)
                if what == "next":
                    act.wait_ge(s["w3_full"], t.n * 5 + 3)
                    if not t.first:
                        act.wait_ge(s["xl_done"], t.n)
                    act.activation(x3T[:], W3[:, 0:TB], ACT.Copy).then_inc(s["w3_free"], 1)
                    act.wait_ge(s["w3_free"], t.n * 5 + 3)
                    act.activation(keep["xh"][:, ds(t.n * TB, TB)], x3T[:], ACT.Copy).then_inc(s["xh_done"], 1)
                if what == "router":
                    act.wait_ge(s["ld_done"], t.n + 1)
                    act.activation(le[:], ld[:], ACT.Exp).then_inc(s["le_done"], 1)
                if what == "gates":
                    act.wait_ge(s["w3_full"], t.n * 5 + 5)
                    if not t.first:
                        act.wait_ge(s["sent"], t.n * 32)
                    act.activation(gT[:], W3[0:2 * E, 0:P], ACT.Copy).then_inc(s["w3_free"], 1)

            skewed(act, NB, parts_of(part))

        @block.vector
        def _(dve):
            ready(dve)
            heads = lambda v: v.rearrange("p a (h e) -> p a h e", e=HD)

            def part(what, t, k):
                if what == "project":
                    dve.wait_ge(s["high_done"], t.n + 1)
                    if not t.early:
                        dve.wait_ge(s["ss_full"], (t.n - 1) * 4)
                    for out, a in ((qs[t.p], 0), (ks[t.p], 1)):
                        ins = dve.scalar_tensor_tensor(out=out[:], in0=high[:, a], scalar=cols[:, 1 + a:2 + a],
                                                       in1=full[:, a], op0=ALU.mult, op1=ALU.add)
                    ins.then_inc(s["qk_done"], 1)
                if what == "features":
                    q, kk, v = WG[:, :, 0:GW], WG[:, :, GW:2 * GW], WG[:, :, 2 * GW:2 * GW + C]
                    dve.wait_ge(s["wg_full"], t.n + 1)
                    if not t.early:
                        dve.wait_ge(s["mi_full"], (t.n - 1) * 6)
                    c = Tally(dve, s["feat_own"], 3, t.n)
                    dve.tensor_scalar(kn[:], kk, 0.0, None, ALU.min).then_inc(s["kn_done"], 1)
                    c.link(dve.tensor_reduce(qm[:], heads(q), AX.X, ALU.max))
                    dve.tensor_tensor(heads(qd[:]), heads(q), qm[:, :, :, None].to_broadcast([P, 2, GH, HD]),
                                      ALU.subtract).then_inc(s["qd_done"], 1)
                    dve.tensor_copy(gv[t.p][:, :, 0:GW], v[:, :, LH * HD:])
                    dve.tensor_copy(va[t.p][:, :, :, 0:HD], heads(v[:, :, 0:LH * HD]))
                    dve.wait_ge(s["ke_done"], t.n + 1)
                    dve.scalar_tensor_tensor(out=kf[t.p][:], in0=kk, scalar=0.0, in1=ke[:], op0=ALU.max,
                                             op1=ALU.add).then_inc(s["wg_free"], 1)
                    dve.wait_ge(s["qe_done"], t.n + 1)
                    c.link(dve.tensor_reduce(qsum[:], heads(qe[:]), AX.X, ALU.add))
                    c.link(dve.reciprocal(qr[:], qsum[:]))
                    if not t.first:
                        dve.wait_ge(s["w1_full"], t.n * 3)
                    dve.tensor_tensor(heads(qn[:]), heads(qe[:]), qr[:, :, :, None].to_broadcast([P, 2, GH, HD]),
                                      ALU.mult).then_inc(s["qn_done"], 1)
                if what == "scores":
                    dve.wait_ge(s["ss_full"], t.n * 4 + k + 1)
                    c = Tally(dve, s["mx_own"], 2, t.n)
                    c.n = k
                    dve.tensor_reduce(mx[:, k], SS[:].rearrange("p b (h j) -> p (b h) j", h=2)[:, :, 0:P * (k + 1)],
                                      AX.X, ALU.max).then_inc(s["ss_free"], 1)
                    dve.wait_ge(s["ss_free"], t.n * 4 + k + 1)
                    if not t.first:
                        dve.wait_ge(s["mi_full"], t.n * 6 - 5 + 2 * k)
                    c.link(dve.tensor_copy(mpad[:, k, :, 24], mx[:, k]))
                    dve.tensor_tensor(mpad[:, k, :, 25], mx[:, k], mpad[:, k, :, 24],
                                      ALU.subtract).then_inc(s["mpad_done"], 1)
                if what == "shift":
                    dve.wait_ge(s["mi_full"], t.n * 6 + 2 * k + 1)
                    if not t.first:
                        dve.wait_ge(s["ss_full"], t.n * 4 - 1 + k)
                    dve.tensor_tensor(q2[:, k], qs[t.p][:, k * P:(k + 1) * P], MT,
                                      ALU.subtract).then_inc(s["mi_free"], 1)
                if what == "context":
                    cx = MI[0:GW, 0:3 * (GW + 1)].rearrange("p (u e) -> p u e", u=3)
                    dve.wait_ge(s["mi_full"], t.n * 6 + 2)
                    c = Tally(dve, s["ctx_own"], 2, t.n)
                    c.link(dve.tensor_scalar(den[:], cx[:, :, GW], 1e-6, None, ALU.add))
                    c.link(dve.reciprocal(rinv[:], den[:]))
                    if not t.first:
                        dve.wait_ge(s["mi_full"], t.n * 6 - 2)
                    for u in range(3):
                        ins = dve.scalar_tensor_tensor(out=ctxn[:, u], in0=cx[:, u, 0:GW], scalar=rinv[:, u:u + 1],
                                                       in1=same_head[:], op0=ALU.mult, op1=ALU.mult)
                    ins.then_inc(s["mi_free"], 1)
                if what == "linear":
                    dve.wait_ge(s["mi_full"], t.n * 6 + 4)
                    if not t.early:
                        dve.wait_ge(s["w3_full"], (t.n - 1) * 5)
                    dve.tensor_copy(ob[t.p][BK:P, 0, LH * HD:], MI[BK:P, 0:GW])
                    dve.tensor_copy(ob[t.p][:, 1, LH * HD:], MI[:, GW:2 * GW]).then_inc(s["mi_free"], 1)
                if what == "back":
                    o4 = MI[:, 0:P].rearrange("p (h e) -> p h e", e=32)
                    dve.wait_ge(s["mi_full"], t.n * 6 + 5 + k)
                    c = Tally(dve, s["norm_own"], 2, t.n)
                    c.n = k
                    c.link(dve.reciprocal(rc[:, k, :], o4[:, :, HD]))
                    dve.tensor_tensor(ob[t.p][:, k, 0:LH * HD].rearrange("p (h e) -> p h e", e=HD),
                                      o4[:, :, 0:HD], rc[:, k, :, None].to_broadcast([P, LH, HD]),
                                      ALU.mult).then_inc(s["mi_free"], 1)
                if what == "mix":
                    dve.wait_ge(s["w3_full"], t.n * 5 + 2)
                    dve.wait_ge(s["xb_done"], t.n + 1)
                    dve.tensor_tensor(r[:], W3[:, 0:TB].rearrange("p (a c) -> p a c", a=2), xb[t.p][:],
                                      ALU.add).then_inc(s["w3_free"], 1)
                    dve.wait_ge(s["w3_free"], t.n * 5 + 2)
                    c = Tally(dve, s["r_own"], 4, t.n)
                    for a in range(2):
                        c.inc(dve.bn_stats(st[:, a, :], r[:, a, :]))
                    c.wait()
                    settle(dve, s["passed_dve"])
                    c.inc(dve.bn_aggr(mv[:, 0, :], st[:, 0, :]))
                    dve.bn_aggr(mv[:, 1, :], st[:, 1, :]).then_inc(s["var_done"], 1)
                    if not t.first:
                        dve.wait_ge(s["xa_done"], t.n)
                        dve.wait_ge(s["w3_full"], t.n * 5)
                    dve.wait_ge(s["rstd_done"], t.n + 1)
                    for a in range(2):
                        ins = dve.tensor_scalar(xn[:, a, :], r[:, a, :], mv[:, a, 0:1], rstd[:, a:a + 1],
                                                ALU.subtract, ALU.mult)
                        ins.then_inc(s["xn_done"], 1) if a else c.inc(ins)
                if what == "next":
                    dve.wait_ge(s["xh_done"], t.n + 1)
                    xh = keep["xh"][:, ds(t.n * TB, TB)]
                    dve.tensor_tensor(keep["xl"][:, ds(t.n * TB, TB)], x3T[:], xh.bitcast(F32),
                                      ALU.subtract).then_inc(s["xl_done"], 1)
                if what == "router":
                    dve.wait_ge(s["w3_full"], t.n * 5 + 4)
                    c = Tally(dve, s["lg_own"], 8, t.n)
                    dve.tensor_copy(lg[:], W3[:, 0:2 * E].rearrange("p (a e) -> p a e", a=2)).then_inc(s["w3_free"], 1)
                    dve.wait_ge(s["w3_free"], t.n * 5 + 4)
                    c.link(dve.tensor_reduce(lm[:], lg[:], AX.X, ALU.max))
                    dve.tensor_tensor(ld[:], lg[:], lm[:, :, None].to_broadcast([P, 2, E]),
                                      ALU.subtract).then_inc(s["ld_done"], 1)
                    other = lg[:, :, None, :].to_broadcast([P, 2, E, E])
                    own = lg[:, :, :, None].to_broadcast([P, 2, E, E])
                    c.inc(dve.tensor_tensor(gtr[:], other, own, ALU.is_gt))
                    c.link(dve.tensor_tensor(eqr[:], other, own, ALU.is_equal))
                    c.link(dve.tensor_tensor(eqr[:], eqr[:], before[:, None, :, :].to_broadcast([P, 2, E, E]),
                                             ALU.mult))
                    c.link(dve.tensor_tensor(gtr[:], gtr[:], eqr[:], ALU.add))
                    c.link(dve.tensor_reduce(rank[:], gtr[:], AX.X, ALU.add))
                    dve.wait_ge(s["le_done"], t.n + 1)
                    c.link(dve.scalar_tensor_tensor(out=sel[:], in0=rank[:], scalar=2.0, in1=le[:],
                                                    op0=ALU.is_lt, op1=ALU.mult))
                    c.link(dve.tensor_reduce(gsum[:], sel[:], AX.X, ALU.add))
                if what == "gates":
                    c = Tally(dve, s["lg_own"], 8, t.n)
                    c.n = 8
                    dve.reciprocal(grec[:], gsum[:]).then_inc(s["o_done"], 1)
                    dve.wait_ge(s["o_done"], t.n + 1)
                    if not t.first:
                        dve.wait_ge(s["w3_full"], t.n * 5)
                    dve.tensor_tensor(gt[:], sel[:], grec[:, :, None].to_broadcast([P, 2, E]),
                                      ALU.mult).then_inc(s["gt_done"], 1)

            skewed(dve, NB, parts_of(part))

        @block.tensor
        def _(pe):
            ready(pe)

            def job(full, free, per, t, k):
                if not (t.first and k == 0):
                    pe.wait_ge(s[free], t.n * per + k)
                return lambda ins: ins.then_inc(s[full], 1)

            def heads_in_turn(product, mask, n, count):
                for hb in range(2):
                    if hb:
                        ins.then_inc(s["first_heads"], 1)
                        pe.wait_ge(s["first_heads"], count)
                    for b in range(2):
                        product(2 * b + hb, SS[:, b, hb * 2 * P:hb * 2 * P + n], hb == 0)
                    for b in range(2):
                        ins = pe.matmul(SS[:, b, hb * 2 * P:hb * 2 * P + n], identb[:], mask, start=False,
                                        stop=(hb == 1), skip_group_check=True)
                return ins

            def part(what, t, k):
                if what == "xT":
                    done = job("w1_full", "w1_free", 3, t, 0)
                    pe.wait_ge(s["copied"], t.n + 1)
                    for a in range(2):
                        ins = pe.transpose(W1[:, a * P:(a + 1) * P], xs[t.p][:, a, :], keep["ident"][:])
                    done(ins)
                if what == "project":
                    done = job("w1_full", "w1_free", 3, t, 1)
                    pe.matmul(W1[:, 0:TB], wql[:], xT[:], start=True, stop=True)
                    done(pe.matmul(W1[:, TB:2 * TB], wkl[:], xT[:], start=True, stop=True))
                    done = job("wg_full", "wg_free", 1, t, 0)
                    for a in range(2):
                        ins = pe.matmul(WG[:, a, 0:2 * GW + C], xT[:, a * P:(a + 1) * P], wg[:],
                                        start=True, stop=True)
                    done(ins)
                if what == "qT":
                    done = job("w1_full", "w1_free", 3, t, 2)
                    pe.wait_ge(s["qn_done"], t.n + 1)
                    for a in range(2):
                        ins = pe.transpose(W1[0:GW, a * P:(a + 1) * P], qn[:, a, :], keep["ident"][:])
                    done(ins)
                if what == "scores":
                    pe.wait_ge(s["qk_done"], t.n + 1)
                    done = job("ss_full", "ss_free", 4, t, k)
                    n = P * (k + 1)

                    def product(g, dst, first):
                        rows = slice(32 * g, 32 * g + 32)
                        pe.matmul(dst, qs[t.p][rows, k * P:(k + 1) * P], ks[t.p][rows, 0:n], start=first,
                                  stop=False, skip_group_check=True)

                    done(heads_in_turn(product, causal[:, 1 - k:2, :], n, t.n * 4 + k + 1))
                if what == "shift":
                    done = job("mi_full", "mi_free", 6, t, 2 * k)
                    pe.wait_ge(s["mpad_done"], t.n * 2 + k + 1)
                    done(pe.transpose(MT, mpad[:, k].rearrange("p g r -> p (g r)"), ident16[:]))
                if what == "weights":
                    pe.wait_ge(s["mi_free"], t.n * 6 + 2 * k + 1)
                    done = job("ss_full", "ss_free", 4, t, 2 + k)

                    def product(g, dst, first):
                        rows = slice(32 * g, 32 * g + 32)
                        for w in range(k + 1):
                            pe.matmul(dst[:, w * P:(w + 1) * P], ks[t.p][rows, w * P:(w + 1) * P], q2[rows, k],
                                      start=first and w == 0, stop=False, skip_group_check=True)

                    done(heads_in_turn(product, causalT[:, 1 - k:2, :], P * (k + 1),
                                       t.n * 4 + 3 + k))
                if what == "values":
                    pe.wait_ge(s["ss_free"], t.n * 4 + 3 + k)
                    if k or not t.first:
                        pe.wait_ge(s["ot_free"], t.n * 2 + k)
                    for g in range(LH):
                        for w in range(k + 1):
                            ins = pe.matmul(OT[32 * g:32 * g + 32, k * P:(k + 1) * P], va[t.p][:, w, g, :],
                                            pt[:, k, g, w * P:(w + 1) * P],
                                            start=(w == 0), stop=(w == k))
                    ins.then_inc(s["pv_done"], 1)
                if what == "context":
                    done = job("mi_full", "mi_free", 6, t, 1)
                    pe.wait_ge(s["wg_free"], t.n + 1)
                    n = GW + 1
                    dst = [MI[0:GW, u * n:(u + 1) * n] for u in range(3)]
                    kf_, gv_ = kf[t.p], gv[t.p]
                    pe.matmul(dst[0], kf_[0:BK, 0], gv_[0:BK, 0], start=True, stop=True)
                    pe.matmul(dst[1], kf_[:, 0], gv_[:, 0], start=True, stop=True)
                    pe.matmul(dst[2], kf_[:, 0], gv_[:, 0], start=True, stop=False)
                    done(pe.matmul(dst[2], kf_[0:BK, 1], gv_[0:BK, 1], start=False, stop=True))
                if what == "linear":
                    done = job("mi_full", "mi_free", 6, t, 3)
                    pe.wait_ge(s["w1_free"], t.n * 3 + 3)
                    for b in range(1, 4):
                        a, v = b // 2, b % 2
                        ins = pe.matmul(MI[v * BK:(v + 1) * BK, a * GW:(a + 1) * GW],
                                        qT[t.p][:, b * BK:(b + 1) * BK], ctxn[:, b - 1], start=True, stop=True)
                    done(ins)
                if what == "back":
                    done = job("mi_full", "mi_free", 6, t, 4 + k)
                    pe.wait_ge(s["ot_free"], t.n * 2 + k + 1)
                    done(pe.transpose(MI[:, 0:P], ots[:, k], keep["ident"][:]))
                if what == "mix":
                    done = job("w3_full", "w3_free", 5, t, 0)
                    pe.wait_ge(s["mi_free"], t.n * 6 + 6)
                    for a in range(2):
                        ins = pe.transpose(W3[:, a * P:(a + 1) * P], ob[t.p][:, a, :], keep["ident"][:])
                    done(ins)
                    done = job("w3_full", "w3_free", 5, t, 1)
                    for a in range(2):
                        ins = pe.matmul(W3[:, a * P:(a + 1) * P], aT[:, a * P:(a + 1) * P], wo[:],
                                        start=True, stop=True)
                    done(ins)
                if what == "next":
                    done = job("w3_full", "w3_free", 5, t, 2)
                    pe.wait_ge(s["xn_done"], t.n + 1)
                    for a in range(2):
                        ins = pe.transpose(W3[:, a * P:(a + 1) * P], xn[:, a, :], keep["ident"][:])
                    done(ins)
                if what == "router":
                    done = job("w3_full", "w3_free", 5, t, 3)
                    for a in range(2):
                        ins = pe.matmul(W3[:, a * E:(a + 1) * E], x3T[:, a * P:(a + 1) * P], gate1[:],
                                        start=True, stop=True)
                    done(ins)
                if what == "gates":
                    done = job("w3_full", "w3_free", 5, t, 4)
                    pe.wait_ge(s["gt_done"], t.n + 1)
                    done(pe.transpose(W3[0:2 * E, 0:P], gt[:].rearrange("p a e -> p (a e)"), keep["ident"][:]))

            skewed(pe, NB, parts_of(part))


def program(nc, d, out):
    gates0 = nc.dram_tensor("gates0", [E, T], F32, kind="Internal").ap()
    gates1 = nc.dram_tensor("gates1", [E, T], F32, kind="Internal").ap()
    with ExitStack() as ctx:
        m = Mem(nc, ctx, "keep")
        keep = {"ident": m.sb("ident", [P, P]), "gate0": m.sb("gate0", [P, E]),
                "xh": m.sb("xh", [P, T], F32R), "xl": m.sb("xl", [P, T], F32R),
                "xa": m.sb("xa", [P, NT, C]), "logits": m.sb("logits", [P, NT, E])}
        with ExitStack() as c2:
            m2 = Mem(nc, c2, "early")
            keep["x1"], keep["xs"] = m2.sb("x1", [P, NT, C]), m2.sb("xs", [P, NT, C])
            attention_0(nc, d, keep)
            for n in ("w1h", "w1l", "w2h", "w2l"):
                keep[n] = m2.sb(n, [P, FB * P], F32R)
            split_weights(nc, "wm", keep, d["m_w1"], d["m_w2"])
            sub = {"b1": d["m_b1"], "cols": d["m_cols"], "b2": d["m_b2"]}
            experts(nc, "m", keep, sub, 1, ACT.Gelu, norm_first=True, transposed=True)
        with ExitStack() as c2:
            m2 = Mem(nc, c2, "late")
            for n in ("w1h", "w1l", "w2h", "w2l"):
                keep[n] = m2.sb(n, [P, E * FB * P], F32R)
            threshold(nc, keep, gates0)
            split_weights(nc, "w0", keep, d["e0_w1"], d["e0_w2"])
            sub = {"b1": d["e0_b1"], "cols": d["m_cols"], "b2": d["e0_b2"]}
            experts(nc, "e0", keep, sub, E, ACT.Gelu_apprx_tanh, gates=gates0)
            attention_1(nc, d, keep, gates1)
            split_weights(nc, "w1", keep, d["e1_w1"], d["e1_w2"])
            sub = {"b1": d["e1_b1"], "cols": d["m_cols"], "b2": d["e1_b2"]}
            experts(nc, "e1", keep, sub, E, ACT.Gelu, gates=gates1, out=out)


def heads_to_rows(w, rows, one_rows=False):
    import numpy as np
    lead = w.shape[:-1]
    out = np.zeros(lead + (rows, 4, 32), w.dtype)
    v = w.reshape(lead + (rows, 4, HD))
    for r in range(3):
        out[..., HD * r:HD * r + HD] = v
    if one_rows:
        out[..., 24:26] = 1.0
    return out.reshape(lead + (rows, P))


def constants():
    import numpy as np
    bf16 = mybir.dt.np(BF16)
    c = {}
    c["ident"] = np.eye(P, dtype=np.float32)
    c["ident16"] = np.eye(P, dtype=np.float16)
    c["identb"] = np.eye(P, dtype=bf16)
    i, j = np.arange(P)[:, None] % BK, np.arange(P)[None, :]
    mask = np.where((j < BK) | (j - BK <= i), 0.0, NEG)
    c["causal64"] = np.repeat(mask[:, None, :], 4, 1).astype(bf16)
    k = np.zeros((P, 4, BK), np.float16)
    for r in (24, 25):
        k[r::32] = 1.0
    c["kpad"] = k
    i, j = np.arange(P)[:, None], np.arange(P)[None, :]
    z = np.zeros((P, P))
    c["causal128"] = np.stack([z, np.where(j <= i, 0.0, NEG)], 1).astype(bf16)
    c["causal128T"] = np.stack([z, np.where(i <= j, 0.0, NEG)], 1).astype(bf16)
    h = np.arange(GW) // HD
    c["same_head"] = (h[:, None] == h[None, :]).astype(np.float32)
    e = np.arange(E)
    c["before"] = np.ascontiguousarray(np.broadcast_to(e[None, :] < e[:, None], (P, E, E))).astype(np.float32)
    low = np.zeros((P, 2), np.float32)
    for g in range(4):
        low[32 * g + 16:32 * g + 24, 0] = -1.0
        low[32 * g + 8:32 * g + 16, 1] = -1.0
    c["low"] = low
    return c


def layout(a):
    import numpy as np
    c = constants()
    out = {k: v for k, v in c.items() if k != "low"}
    out["x"] = a["L0_attn_x"]
    w, b = a["L0_attn_w_qkv"], a["L0_attn_b_qkv"]
    out["w_q"], out["w_k"] = heads_to_rows(w[:, :C], 4), heads_to_rows(w[:, C:2 * C], 4)
    out["w_v"] = np.ascontiguousarray(w[:, 2 * C:])
    out["w_out"] = a["L0_attn_w_out"]
    out["b_out"] = a["L0_attn_b_out"].reshape(1, C)
    cols = np.zeros((P, 16), np.float32)
    cols[:, 0], cols[:, 1] = a["L0_attn_ln1_g"], a["L0_attn_ln1_b"]
    cols[:, 2:6] = heads_to_rows(b[:C], 4).T
    cols[:, 6:10] = heads_to_rows(b[C:2 * C], 4, True).T
    cols[:, 10] = b[2 * C:]
    cols[:, 11:13] = c["low"]
    out["cols"] = cols
    up = lambda w: np.ascontiguousarray(w.transpose(2, 0, 1).reshape(C, -1))
    down = lambda w: np.ascontiguousarray(w.reshape(-1, FB, P, C).transpose(2, 0, 1, 3).reshape(P, -1))
    per_row = lambda b: np.ascontiguousarray(b.reshape(-1, P).T)
    out["m_w1"] = a["L0_attn_w1"]
    out["m_w2"] = down(a["L0_attn_w2"][None])
    out["m_b1"] = per_row(a["L0_attn_b1"])
    out["m_b2"] = a["L0_attn_b2"].reshape(1, C)
    mc = np.zeros((P, 4), np.float32)
    mc[:, 0], mc[:, 1], mc[:, 2] = a["L0_attn_ln2_g"], a["L0_attn_ln2_b"], a["L0_attn_b2"]
    out["m_cols"] = mc
    out["e0_w1"] = up(a["L0_ffn_w1"])
    out["e0_w2"] = down(a["L0_ffn_w2"].transpose(0, 2, 1))
    out["e0_b1"] = per_row(a["L0_ffn_b1"])
    out["e0_b2"] = a["L0_ffn_b2"]
    out["e1_w1"] = up(a["L1_ffn_w1"].transpose(0, 2, 1))
    out["e1_w2"] = down(a["L1_ffn_w2"])
    out["e1_b1"] = per_row(a["L1_ffn_b1"])
    out["e1_b2"] = a["L1_ffn_b2"]
    wq, wk, wv = a["L1_attn_Wq"], a["L1_attn_Wk"], a["L1_attn_Wv"]
    n = LH * HD
    out["b_wql"], out["b_wkl"] = heads_to_rows(wq[:, :n], 1)[:, 0], heads_to_rows(wk[:, :n], 1)[:, 0]
    out["b_wg"] = np.concatenate([wq[:, n:], wk[:, n:], wv], 1)
    out["b_wo"] = a["L1_attn_Wo"]
    out["b_bo"] = a["L1_attn_bo"].reshape(1, C)
    bc = np.zeros((P, 4), np.float32)
    bc[24::32, 0] = bc[25::32, 0] = 1.0
    bc[:, 1:3] = c["low"]
    out["b_cols"] = bc
    out["gate1"] = a["L1_ffn_gate_w"]
    out["gate0"] = np.ascontiguousarray(a["L0_ffn_gate_weight"].T)
    return out


def kernel(**inputs):
    import numpy as np
    import concourse.bacc as bacc
    from concourse.bass_utils import run_bass_kernel_spmd

    nc = bacc.Bacc("TRN2", target_bir_lowering=False, num_devices=1)
    arrays, d = {}, {}
    for name, a in layout({k: np.asarray(v) for k, v in inputs.items()}).items():
        a = np.ascontiguousarray(a)
        arrays[name] = a
        d[name] = nc.dram_tensor(name, a.shape, mybir.dt.from_np(a.dtype), kind="ExternalInput").ap()
    tokens = "s (t p) c -> p (s t) c"
    d["x"] = d["x"].rearrange(tokens, p=P)
    out = nc.dram_tensor("out", (NB, TB, C), F32, kind="ExternalOutput").ap()
    program(nc, d, out.rearrange(tokens, p=P))
    return run_bass_kernel_spmd(nc, [arrays], core_ids=[0]).results[0]["out"]
```

```python
import concourse.bass as bass
from concourse import mybir
from contextlib import ExitStack

P = 128
NB, TB, C = 16, 256, 128
T = NB * TB
NT = T // P
H, HD = 16, 8
BK = 64
E, F = 8, 512
FB = F // P
CT = 512
NC_ = T // CT
EPS = 1e-5
NEG = -1e30
KEEP_FROM = 4 * 128 * 6

ALU = mybir.AluOpType
ACT = mybir.ActivationFunctionType
AX = mybir.AxisListType
F32 = mybir.dt.float32
F32R = mybir.dt.float32r
F16 = mybir.dt.float16
BF16 = mybir.dt.bfloat16
U32 = mybir.dt.uint32
ds = bass.ds


class Tally:

    def __init__(self, eng, sem, per, b):
        self.eng, self.sem, self.per, self.b, self.n = eng, sem, per, b, 0

    def inc(self, ins):
        ins.then_inc(self.sem, 1)
        self.n += 1

    def wait(self):
        self.eng.wait_ge(self.sem, self.b * self.per + self.n)

    def link(self, ins):
        self.inc(ins)
        self.wait()


class Turn:

    def __init__(self, i, off):
        self.n, self.p, self.half = i * 2 + off, off % 2, i + off // 2
        self.first = isinstance(i, int) and i * 2 + off < 1
        self.early = isinstance(i, int) and i * 2 + off < 2


def wait(eng, sem, value):
    if isinstance(value, int) and value <= 0:
        return
    eng.wait_ge(sem, value)


def settle(eng, passed):
    eng.sem_inc(passed, 1)


class Mem:

    def __init__(self, nc, ctx, tag):
        self.nc, self.ctx, self.tag, self.sems = nc, ctx, tag, []
        ctx.callback(self.clear)

    def clear(self):
        if self.sems:
            self.nc.clear_and_free_semaphores(self.sems)
            self.nc.all_engine_barrier()

    def sb(self, name, shape, dt=F32):
        return self.ctx.enter_context(self.nc.sbuf_tensor(f"{self.tag}__{name}", shape, dt))

    def ps(self, name, shape, dt=F32):
        return self.ctx.enter_context(self.nc.psum_tensor(f"{self.tag}__{name}", shape, dt))

    def sem(self, name):
        self.sems.append(self.nc.alloc_semaphore(f"{self.tag}__{name}"))
        return self.sems[-1]


PACKS = {
    "a32": (F32, (("wq", (P,)), ("wk", (P,)), ("wv", (P,)), ("wo", (P,)), ("cols", (6,)))),
    "a16": (F16, (("spread", (4, 4, P)), ("ident16", (P,)))),
    "abf": (BF16, (("identb", (P,)), ("causal", (4, P)))),
    "b32": (F32, (("wql", (P,)), ("wkl", (P,)), ("wg", (2 * 96 + C,)), ("wo", (P,)), ("cols", (4,)),
                  ("same_head", (96,)), ("before", (E, E)), ("gate1", (E,)))),
    "b16": (F16, (("ident16", (P,)),)),
    "bbf": (BF16, (("identb", (P,)), ("causal", (2, P)), ("causalT", (2, P)))),
}


def numbers(shape):
    n = 1
    for v in shape:
        n *= v
    return n


def unpacked(m, name):
    dt, parts = PACKS[name]
    whole = m.sb(name, [P, sum(numbers(shape) for _, shape in parts)], dt)
    at, views = 0, {}
    for part, shape in parts:
        v = whole[:, at:at + numbers(shape)]
        at += numbers(shape)
        if len(shape) == 2:
            v = v.rearrange("p (a b) -> p a b", a=shape[0])
        if len(shape) == 3:
            v = v.rearrange("p (a b c) -> p a b c", a=shape[0], b=shape[1])
        views[part] = v
    return whole, views


class Split:

    def __init__(self, m, keep, w1, w2):
        n = w1.shape[1]
        size = min(n, 2048)
        self.stage = m.sb("stage", [P, 2, size])
        self.landed = [m.sem("landed0"), m.sem("landed1")]
        self.high_done, self.low_done = m.sem("split_high"), m.sem("split_low")
        self.parts = []
        for src, high, low in ((w1, keep["w1h"], keep["w1l"]), (w2, keep["w2h"], keep["w2l"])):
            for c in range(n // size):
                s = slice(c * size, (c + 1) * size)
                self.parts.append((src[:, s], high[:, s], low[:, s]))

    def load(self, sp):
        for c, (src, _, _) in enumerate(self.parts):
            wait(sp, self.low_done, c - 1)
            sp.dma_start(self.stage[:, c % 2], src).then_inc(self.landed[c % 2], 16)

    def high(self, act):
        for c, (_, high, _) in enumerate(self.parts):
            act.wait_ge(self.landed[c % 2], 16 * (c // 2 + 1))
            act.activation(high, self.stage[:, c % 2], ACT.Copy).then_inc(self.high_done, 1)

    def low(self, eng):
        for c, (_, high, low) in enumerate(self.parts):
            eng.wait_ge(self.high_done, c + 1)
            eng.tensor_tensor(low, self.stage[:, c % 2], high.bitcast(F32),
                              ALU.subtract).then_inc(self.low_done, 1)


def skewed(eng, n, step):
    step(Turn(0, 0), None, None)
    step(Turn(0, 1), Turn(0, 0), None)
    with eng.Fori(0, n // 2 - 1) as i:
        for off in (1, 2):
            step(Turn(i, off + 1), Turn(i, off), Turn(i, off - 1))
    last = n // 2 - 1
    step(None, Turn(last, 1), Turn(last, 0))
    step(None, None, Turn(last, 1))


ORDER_0 = [("scores", 0), ("turn", 0), ("output", 0), ("shift", 0), ("stats", 0), ("norm", 0),
           ("scores", 1), ("weights", 0), ("weights", 1), ("hT", 0), ("qk", 0), ("weights", 2),
           ("shift", 1), ("values", 0), ("proj", 0), ("weights", 3), ("values", 1), ("weights", 4),
           ("values", 2), ("proj", 1), ("weights", 5), ("weights", 6), ("values", 3), ("proj", 2),
           ("back", 0), ("weights", 7), ("proj", 3), ("values", 4), ("vT", 0), ("values", 5),
           ("values", 6), ("values", 7), ("windows", 0), ("back", 1)]


def attention_0(nc, d, keep, w1, w2):
    with ExitStack() as ctx:
        m = Mem(nc, ctx, "a")
        (a32, f32), (a16, f16), (abf, bf16) = (unpacked(m, n) for n in ("a32", "a16", "abf"))
        wq, wk, wv, wo = f32["wq"], f32["wk"], f32["wv"], f32["wo"]
        cols = f32["cols"]
        spread = f16["spread"]
        ident, ident16, identb, causal = keep["ident"], f16["ident16"], bf16["identb"], bf16["causal"]
        bo = m.sb("bo", [P, P])
        x = m.sb("x", [P, NT, C])
        st = m.sb("st", [P, 2, 6])
        mv = m.sb("mv", [P, 2, 2])
        half = m.sb("half", [P, 2])
        rstd = m.sb("rstd", [P, 2])
        hn = m.sb("hn", [P, 2, C])
        hT = m.sb("hT", [P, TB])
        high = m.sb("high", [P, 2, TB], F16)
        low = m.sb("low", [P, 2, TB], F16)
        qs = [m.sb(f"qs{p}", [P, 4, TB], F16) for p in range(2)]
        ks = [m.sb(f"ks{p}", [P, 4, BK + TB], F16) for p in range(2)]
        vT = m.sb("vT", [P, BK + TB])
        va = [m.sb(f"va{p}", [P, 4, H, 32]) for p in range(2)]
        mx = m.sb("mx", [P, 2, 4, 4])
        mpad = m.sb("mpad", [P, 2, 4, 4, 32], F16)
        q2 = m.sb("q2", [P, 2, 4, P], F16)
        pt = m.sb("pt", [P, 4, 512])
        ots = m.sb("ots", [P, 2, 512])
        rc = m.sb("rc", [P, 2, H])
        ob = [m.sb(f"ob{p}", [P, 2, C]) for p in range(2)]
        aT = m.sb("aT", [P, TB])

        S = m.ps("S", [P, 2, 512])
        ST = m.ps("ST", [P, 2, 512])
        OT = m.ps("OT", [P, 512])
        MI = m.ps("MI", [P, 512])
        W1 = m.ps("W1", [P, 512])
        W3 = m.ps("W3", [P, 512])
        MT = MI[:, 0:256].bitcast(F16).rearrange("p (a b) -> p a b", a=4)

        loaded = m.sem("loaded")
        cleared = m.sem("cleared")
        x_first, x_rest = m.sem("x_first"), m.sem("x_rest")
        xb_done = m.sem("xb_done")
        ln = m.sem("ln")
        var_done = m.sem("var_done")
        rstd_done = m.sem("rstd_done")
        pool_ln = m.sem("pool_ln")
        passed_pool, passed_dve = m.sem("passed_pool"), m.sem("passed_dve")
        hn_done = m.sem("hn_done")
        w1_full = m.sem("w1_full")
        w1_free = m.sem("w1_free")
        high_done = m.sem("high_done")
        s_full = m.sem("s_full")
        s_free = m.sem("s_free")
        mx_own = m.sem("mx_own")
        mpad_done = m.sem("mpad_done")
        mi_full = m.sem("mi_full")
        mi_free = m.sem("mi_free")
        st_full = m.sem("st_full")
        exp_done = m.sem("exp_done")
        causal_done = m.sem("causal_done")
        pv_done = m.sem("pv_done")
        ot_free = m.sem("ot_free")
        norm_own = m.sem("norm_own")
        w3_full = m.sem("w3_full")
        w3_free = m.sem("w3_free")
        x1_own = m.sem("x1_own")
        x1_done = m.sem("x1_done")
        LOADS = 8
        split = Split(m, keep, w1, w2)

        def rows_landed(eng, turn):
            eng.wait_ge(x_first if isinstance(turn.n, int) and turn.n < 2 else x_rest, 16)

        def rows(turn, a):
            return x[:, ds(turn.n * 2 + a, 1), :].rearrange("p a c -> p (a c)")

        g1, s1 = cols[:, 0:1], cols[:, 1:2]
        scale = float(HD) ** -0.5
        block = ctx.enter_context(nc.Block())

        @block.sync
        def _(sp):
            sp.dma_start(x[:, 0:4, :], d["x"][:, 0:4, :]).then_inc(x_first, 16)
            for dst, src in ((a32[:], d["a32"]), (ident[:], d["ident"]), (a16[:], d["a16"]), (abf[:], d["abf"]),
                             (bo[:], d["b_out"].to_broadcast([P, C])),
                             (ks[0][:, :, 0:BK], d["kpad"]), (ks[1][:, :, 0:BK], d["kpad"]),
                             (keep["gate0"][:], d["gate0"])):
                sp.dma_start(dst, src).then_inc(loaded, 16)
            sp.dma_start(x[:, 4:NT, :], d["x"][:, 4:NT, :]).then_inc(x_rest, 16)
            split.load(sp)

        @block.gpsimd
        def _(pool):
            pool.memset(half[:], -0.5)
            pool.memset(va[0][:], 0.0)
            pool.memset(va[1][:], 0.0)
            pool.memset(vT[:], 0.0)
            pool.memset(mpad[:], 0.0).then_inc(cleared, 1)
            pool.wait_ge(cleared, 1)
            for v in va:
                pool.memset(v[:, :, :, HD:HD + 1], 1.0).then_inc(cleared, 1)
            pool.wait_ge(cleared, 3)
            pool.wait_ge(loaded, 16 * LOADS)

            def step(pre, main, post):
                for what, k in ORDER_0:
                    if what == "stats" and pre:
                        pool.wait_ge(var_done, pre.n + 1)
                        settle(pool, passed_pool)
                        t = Tally(pool, pool_ln, 1, pre.n)
                        t.link(pool.tensor_scalar(rstd[:], mv[:, :, 1], EPS, 1.0, ALU.add, ALU.mult))
                        pool.tensor_tensor(rstd[:], rstd[:], half[:], ALU.pow).then_inc(rstd_done, 1)
                    if what == "norm" and pre:
                        rows_landed(pool, pre)
                        for t in range(2):
                            xb = keep["xs"][:, ds(pre.n * 2 + t, 1), :].rearrange("p a c -> p (a c)")
                            ins = pool.tensor_tensor(xb, rows(pre, t), bo[:], ALU.add)
                        ins.then_inc(xb_done, 1)
                    if what == "weights" and main:
                        pool.wait_ge(exp_done, main.n * 8 + k + 1)
                        settle(pool, passed_pool)
                        v = pt[:, k % 4, :].rearrange("p (a i) -> p a i", a=8)
                        pool.affine_select(out=v, in_=v, compare_op=ALU.is_ge, fill=0.0, base=BK,
                                           pattern=[[0, 8], [1, BK]],
                                           channel_multiplier=-1).then_inc(causal_done, 1)

            skewed(pool, NB, step)
            split.low(pool)

        @block.scalar
        def _(act):
            act.wait_ge(loaded, 16 * LOADS)
            act.wait_ge(cleared, 3)

            def step(pre, main, post):
                for what, k in ORDER_0:
                    if what == "hT" and pre:
                        act.wait_ge(w1_full, pre.n * 8 + 1)
                        act.activation(hT[:], W1[:, 0:TB], ACT.Identity, scale=g1, bias=s1).then_inc(w1_free, 1)
                    if what == "qk" and pre:
                        act.wait_ge(w1_full, pre.n * 8 + 2)
                        for a in range(2):
                            ins = act.activation(high[:, a, :], W1[:, a * TB:(a + 1) * TB], ACT.Identity,
                                                 bias=cols[:, 2 + a:3 + a])
                        ins.then_inc(high_done, 1)
                    if what == "proj" and pre:
                        act.wait_ge(w1_full, pre.n * 8 + 3 + k)
                        if not pre.early:
                            act.wait_ge(st_full, (pre.n - 1) * 8)
                        rows2 = W1[:].rearrange("p (a i) -> p a i", a=2)
                        if k < 2:
                            ins = act.activation(qs[pre.p][:, 2 * k:2 * k + 2, :], rows2, ACT.Copy)
                        else:
                            ins = act.activation(ks[pre.p][:, 2 * k - 4:2 * k - 2, BK:BK + TB], rows2,
                                                 ACT.Identity, bias=cols[:, 5:6])
                        ins.then_inc(w1_free, 1)
                    if what == "vT" and pre:
                        act.wait_ge(w1_full, pre.n * 8 + 7)
                        act.activation(vT[:, BK:BK + TB], W1[:, 0:TB], ACT.Identity,
                                       bias=cols[:, 4:5]).then_inc(w1_free, 1)
                    if what == "weights" and main:
                        act.wait_ge(st_full, main.n * 8 + k + 1)
                        if not (main.first and k < 4):
                            act.wait_ge(pv_done, main.n * 8 + k - 3)
                        act.activation(pt[:, k % 4, :], ST[:, k % 2, :], ACT.Exp,
                                       scale=scale).then_inc(exp_done, 1)
                    if what == "back" and main:
                        act.wait_ge(pv_done, main.n * 8 + 4 * k + 4)
                        if not main.first:
                            act.wait_ge(mi_full, main.n * 4 - 1 + k)
                        act.activation(ots[:, k, :], OT[:], ACT.Copy).then_inc(ot_free, 1)
                    if what == "turn" and post:
                        act.wait_ge(w3_full, post.n * 2 + 1)
                        act.activation(aT[:], W3[:, 0:TB], ACT.Copy).then_inc(w3_free, 1)

            skewed(act, NB, step)
            split.high(act)

        @block.vector
        def _(dve):
            dve.wait_ge(loaded, 16 * LOADS)
            dve.wait_ge(cleared, 3)

            def step(pre, main, post):
                for what, k in ORDER_0:
                    if what == "stats" and pre:
                        rows_landed(dve, pre)
                        wait(dve, rstd_done, 0 if pre.first else pre.n)
                        t = Tally(dve, ln, 3, pre.n)
                        for a in range(2):
                            t.inc(dve.bn_stats(st[:, a, :], rows(pre, a)))
                        t.wait()
                        settle(dve, passed_dve)
                        t.inc(dve.bn_aggr(mv[:, 0, :], st[:, 0, :]))
                        dve.bn_aggr(mv[:, 1, :], st[:, 1, :]).then_inc(var_done, 1)
                    if what == "norm" and pre:
                        wait(dve, w1_full, 0 if pre.first else pre.n * 8 - 7)
                        dve.wait_ge(rstd_done, pre.n + 1)
                        dve.tensor_scalar(hn[:, 0, :], rows(pre, 0), mv[:, 0, 0:1], rstd[:, 0:1],
                                          ALU.subtract, ALU.mult)
                        dve.tensor_scalar(hn[:, 1, :], rows(pre, 1), mv[:, 1, 0:1], rstd[:, 1:2],
                                          ALU.subtract, ALU.mult).then_inc(hn_done, 1)
                    if what == "qk" and pre:
                        dve.wait_ge(high_done, pre.n + 1)
                        for a in range(2):
                            ins = dve.scalar_tensor_tensor(out=low[:, a, :], in0=W1[:, a * TB:(a + 1) * TB],
                                                           scalar=cols[:, 2 + a:3 + a], in1=high[:, a, :],
                                                           op0=ALU.add, op1=ALU.subtract)
                        ins.then_inc(w1_free, 1)
                    if what == "windows" and pre:
                        dve.wait_ge(w1_full, pre.n * 8 + 8)
                        wait(dve, pv_done, 0 if pre.early else (pre.n - 1) * 8)
                        for w in range(4):
                            ins = dve.tensor_copy(va[pre.p][:, w, :, 0:HD],
                                                  W1[:, w * P:(w + 1) * P].rearrange("p (h e) -> p h e", h=H))
                        ins.then_inc(w1_free, 1)
                    if what == "scores" and main:
                        for g in range(4):
                            u = 4 * k + g
                            dve.wait_ge(s_full, main.n * 8 + u + 1)
                            dve.tensor_reduce(mx[:, k, :, g], S[:, u % 2, :].rearrange("p (a j) -> p a j", a=4),
                                              AX.X, ALU.max).then_inc(s_free, 1)
                        dve.wait_ge(s_free, main.n * 8 + 4 * k + 4)
                        wait(dve, mi_full, 0 if main.first else main.n * 4 - 3 + k)
                        t = Tally(dve, mx_own, 2, main.n)
                        t.n = k
                        t.link(dve.tensor_copy(mpad[:, k, :, :, 24], mx[:, k]))
                        dve.tensor_tensor(mpad[:, k, :, :, 25], mx[:, k], mpad[:, k, :, :, 24],
                                          ALU.subtract).then_inc(mpad_done, 1)
                    if what == "shift" and main:
                        dve.wait_ge(mi_full, main.n * 4 + k + 1)
                        wait(dve, st_full, 0 if main.first else main.n * 8 - 4 + 4 * k)
                        dve.tensor_tensor(q2[:, k], qs[main.p][:, :, k * P:(k + 1) * P], MT,
                                          ALU.subtract).then_inc(mi_free, 1)
                    if what == "back" and main:
                        o4 = MI[:].rearrange("p (h e) -> p h e", e=32)
                        dve.wait_ge(mi_full, main.n * 4 + 3 + k)
                        t = Tally(dve, norm_own, 2, main.n)
                        t.n = k
                        t.link(dve.reciprocal(rc[:, k, :], o4[:, :, HD]))
                        ins = dve.tensor_tensor(ob[main.p][:, k, :].rearrange("p (h e) -> p h e", h=H),
                                                o4[:, :, 0:HD], rc[:, k, :, None].to_broadcast([P, H, HD]),
                                                ALU.mult)
                        ins.then_inc(mi_free, 1)
                    if what == "output" and post:
                        dve.wait_ge(w3_full, post.n * 2 + 2)
                        dve.wait_ge(xb_done, post.n + 1)
                        t = Tally(dve, x1_own, 1, post.n)
                        x1 = keep["x1"][:, ds(post.n * 2, 2), :]
                        xs = keep["xs"][:, ds(post.n * 2, 2), :]
                        t.inc(dve.tensor_tensor(x1, W3[:, 0:TB].rearrange("p (t c) -> p t c", t=2),
                                                xs, ALU.add))
                        t.wait()
                        ins = dve.tensor_tensor(xs, x1, x[:, ds(post.n * 2, 2), :], ALU.add)
                        ins.then_inc(x1_done, 1)

            skewed(dve, NB, step)

        @block.tensor
        def _(pe):
            pe.wait_ge(loaded, 16 * LOADS)
            pe.wait_ge(cleared, 3)

            def step(pre, main, post):
                def job1(k):
                    if not (pre.first and k == 0):
                        pe.wait_ge(w1_free, pre.n * 8 + k)

                for what, k in ORDER_0:
                    if what == "hT" and pre:
                        job1(0)
                        pe.wait_ge(hn_done, pre.n + 1)
                        for a in range(2):
                            ins = pe.transpose(W1[:, a * P:(a + 1) * P], hn[:, a, :], ident[:])
                        ins.then_inc(w1_full, 1)
                    if what == "qk" and pre:
                        job1(1)
                        pe.matmul(W1[:, 0:TB], wq[:], hT[:], start=True, stop=True)
                        pe.matmul(W1[:, TB:2 * TB], wk[:], hT[:], start=True, stop=True).then_inc(w1_full, 1)
                    if what == "proj" and pre:
                        job1(2 + k)
                        for a in range(2):
                            dst, g, w = W1[:, a * TB:(a + 1) * TB], 2 * (k % 2) + a, k // 2
                            pe.matmul(dst, spread[:, 2 * w, g, :], high[:, w, :], start=True, stop=False)
                            ins = pe.matmul(dst, spread[:, 2 * w + 1, g, :], low[:, w, :], start=False, stop=True)
                        ins.then_inc(w1_full, 1)
                    if what == "vT" and pre:
                        job1(6)
                        pe.matmul(W1[:, 0:TB], wv[:], hT[:], start=True, stop=True).then_inc(w1_full, 1)
                    if what == "windows" and pre:
                        job1(7)
                        for w in range(4):
                            ins = pe.transpose(W1[:, w * P:(w + 1) * P], vT[:, w * BK:w * BK + P], ident[:])
                        ins.then_inc(w1_full, 1)
                    if what == "scores" and main:
                        pe.wait_ge(w1_free, main.n * 8 + 6)
                        for g in range(4):
                            u = 4 * k + g
                            if not (main.first and u < 2):
                                pe.wait_ge(s_free, main.n * 8 + u - 1)
                            r = slice(32 * g, 32 * g + 32)
                            for v in range(2):
                                w = 2 * k + v
                                for a in range(4):
                                    ins = pe.matmul(S[BK * v:BK * v + BK, u % 2, a * P:(a + 1) * P],
                                                    qs[main.p][r, a, w * BK:(w + 1) * BK],
                                                    ks[main.p][r, a, w * BK:w * BK + P],
                                                    start=(a == 0), stop=False, skip_group_check=True)
                            ins = pe.matmul(S[:, u % 2, :], identb[:], causal[:], start=False, stop=True,
                                            skip_group_check=True)
                            ins.then_inc(s_full, 1)
                    if what == "shift" and main:
                        pe.wait_ge(mpad_done, main.n * 2 + k + 1)
                        if not (main.first and k == 0):
                            pe.wait_ge(mi_free, main.n * 4 + k)
                        for a in range(4):
                            ins = pe.transpose(MT[:, a, :], mpad[:, k, a].rearrange("p g r -> p (g r)"),
                                               ident16[:])
                        ins.then_inc(mi_full, 1)
                    if what == "weights" and main:
                        t, g = k // 4, k % 4
                        pe.wait_ge(mi_free, main.n * 4 + t + 1)
                        if not (main.first and k < 2):
                            pe.wait_ge(exp_done, main.n * 8 + k - 1)
                        r = slice(32 * g, 32 * g + 32)
                        for v in range(2):
                            for a in range(4):
                                ins = pe.matmul(ST[:, k % 2, (4 * v + a) * BK:(4 * v + a + 1) * BK],
                                                ks[main.p][r, a, (2 * t + v) * BK:(2 * t + v) * BK + P],
                                                q2[r, t, a, v * BK:(v + 1) * BK], start=True, stop=True)
                        ins.then_inc(st_full, 1)
                    if what == "values" and main:
                        t, g = k // 4, k % 4
                        if g == 0 and not (main.first and t == 0):
                            pe.wait_ge(ot_free, main.n * 2 + t)
                        if k == 0:
                            pe.wait_ge(w1_free, main.n * 8 + 8)
                        pe.wait_ge(causal_done, main.n * 8 + k + 1)
                        for v in range(2):
                            for a in range(4):
                                ins = pe.matmul(OT[32 * g:32 * g + 32, a * P + v * BK:a * P + (v + 1) * BK],
                                                va[main.p][:, 2 * t + v, 4 * a + g, :],
                                                pt[:, k % 4, (4 * v + a) * BK:(4 * v + a + 1) * BK],
                                                start=True, stop=True)
                        ins.then_inc(pv_done, 1)
                    if what == "back" and main:
                        pe.wait_ge(ot_free, main.n * 2 + k + 1)
                        pe.wait_ge(mi_free, main.n * 4 + 2 + k)
                        for a in range(4):
                            ins = pe.transpose(MI[:, a * P:(a + 1) * P], ots[:, k, a * P:(a + 1) * P], ident[:])
                        ins.then_inc(mi_full, 1)
                    if what == "turn" and post:
                        if not post.first:
                            pe.wait_ge(w3_free, post.n)
                            pe.wait_ge(x1_done, post.n)
                        pe.wait_ge(mi_free, post.n * 4 + 4)
                        for a in range(2):
                            ins = pe.transpose(W3[:, a * P:(a + 1) * P], ob[post.p][:, a, :], ident[:])
                        ins.then_inc(w3_full, 1)
                    if what == "output" and post:
                        pe.wait_ge(w3_free, post.n + 1)
                        for a in range(2):
                            ins = pe.matmul(W3[:, a * P:(a + 1) * P], aT[:, a * P:(a + 1) * P], wo[:],
                                            start=True, stop=True)
                        ins.then_inc(w3_full, 1)

            skewed(pe, NB, step)


ORDER_M = [("post0", ()), ("stats", ()), ("norm", ()), ("hidden", (0, 1)), ("hidden", (2, 3)),
           ("post1", ()), ("down", (0, 1)), ("pre", ()), ("low1", ()), ("down", (2, 3)), ("post2", ()),
           ("low0", ())]



def experts(nc, tag, keep, d, n_exp, gelu, norm_first=False, transposed=False, gates=None, out=None):
    with ExitStack() as ctx:
        m = Mem(nc, ctx, tag)
        E_ = n_exp
        b1 = m.sb("b1", [P, E_ * FB])
        cols = m.sb("cols", [P, 4])
        b2 = m.sb("b2", [E_, C])
        hf = m.sb("hf", [P, 2, FB, CT])
        hh = m.sb("hh", [P, 2, FB, CT], F32R)
        hl = m.sb("hl", [P, 2, FB, CT], F32R)
        acc = m.sb("acc", [P, 2, CT])
        half = m.sb("half", [P, 8])
        st = m.sb("st", [P, 4, 6])
        mv = m.sb("mv", [P, 4, 2])
        rstd = m.sb("rstd", [P, 4])
        r = m.sb("r", [P, 4, C])
        xn = m.sb("xn", [P, 4, C]) if norm_first else r
        if transposed:
            xT = m.sb("xT", [P, CT])
        if norm_first:
            st0 = m.sb("st0", [P, 4, 6])
            mv0 = m.sb("mv0", [P, 4, 2])
            rstd0 = m.sb("rstd0", [P, 4])
            hn = m.sb("hn", [P, 4, C])
            h2 = m.sb("h2", [P, CT])
        else:
            tmp = m.sb("tmp", [P, CT])
            G = [m.sb(f"G{p}", [P, E_, CT]) for p in range(2)]
            g8 = [m.sb(f"g8{p}", [E_, CT]) for p in range(2)]
        HB = m.ps("HB", [P, 4, CT])
        YB = m.ps("YB", [P, 2, CT])
        PB = m.ps("PB", [P, CT])
        QB = m.ps("QB", [P, CT])

        loaded, half_set = m.sem("loaded"), m.sem("half_set")
        g_in = [m.sem(f"g_in{p}") for p in range(2)]
        ln0 = m.sem("ln0")
        var0_done, rstd0_done, pool0 = m.sem("var0_done"), m.sem("rstd0_done"), m.sem("pool0")
        hn_done = m.sem("hn_done")
        qb_full, qb_free = m.sem("qb_full"), m.sem("qb_free")
        xh_done, xl_done = m.sem("xh_done"), m.sem("xl_done")
        h_full, h_free = m.sem("h_full"), m.sem("h_free")
        hi_done, lo_done = m.sem("hi_done"), m.sem("lo_done")
        y_full, y_free = m.sem("y_full"), m.sem("y_free")
        comb = m.sem("comb")
        acc_done = m.sem("acc_done")
        pb_full, pb_free = m.sem("pb_full"), m.sem("pb_free")
        ln1 = m.sem("ln1")
        var_done, rstd_done, pool1 = m.sem("var_done"), m.sem("rstd_done"), m.sem("pool1")
        passed_pool, passed_dve = m.sem("passed_pool"), m.sem("passed_dve")
        xn_done, xa_done = m.sem("xn_done"), m.sem("xa_done")
        xTh_done, xTl_done = m.sem("xTh_done"), m.sem("xTl_done")
        stored = m.sem("stored")
        jobs = 3 if transposed else 1
        loads = [(b1[:], d["b1"]), (cols[:], d["cols"]), (b2[:], d["b2"])]

        ago = min(2, E_)

        def par(turn, e):
            return e % ago

        all_f = tuple(range(FB))
        order = [(what, 0, f) for what, f in ORDER_M]
        if E_ > 1:
            order = [("pre", 0, all_f)]
            for e in range(E_):
                order += [("hidden", e + 1, all_f), ("down", e, all_f)]
                if e == 0:
                    order += [("post0", 0, all_f), ("norm", 0, all_f)]

        def chunk(t, turn):
            return t[:, ds(turn.n * CT, CT)]

        def parts_of(step):
            def go(pre, main, post):
                for what, k, fs in order:
                    ahead = what in ("stats", "pre", "low0") or (what == "hidden" and k == E_)
                    t = pre if ahead else main if what in ("hidden", "down") else post
                    if t:
                        step(what, t, k % E_, fs)
            return go

        block = ctx.enter_context(nc.Block())

        @block.sync
        def _(sp):
            for dst, src in loads:
                sp.dma_start(dst, src).then_inc(loaded, 16)

            def step(what, t, k, fs):
                if what == "pre" and gates is not None:
                    if not t.early:
                        sp.wait_ge(acc_done, t.n - 1)
                    src = gates[:, ds(t.n * CT, CT)]
                    sp.dma_start(g8[t.p][:], src).then_inc(g_in[t.p], 16)
                    sp.dma_start(G[t.p][:], src[None, :, :].to_broadcast([P, E_, CT])).then_inc(g_in[t.p], 16)
                if what == "norm" and out is not None:
                    sp.wait_ge(xn_done, t.n + 1)
                    sp.dma_start(out[:, ds(t.n * 4, 4), :], xn[:]).then_inc(stored, 16)

            skewed(sp, NC_, parts_of(step))
            if out is not None:
                sp.wait_ge(stored, 16 * NC_)

        @block.gpsimd
        def _(pool):
            pool.memset(half[:], -0.5).then_inc(half_set, 1)
            pool.wait_ge(half_set, 1)

            def step(what, t, k, fs):
                if what == "stats":
                    pool.wait_ge(var0_done, t.n + 1)
                    settle(pool, passed_pool)
                    c = Tally(pool, pool0, 1, t.n)
                    c.link(pool.tensor_scalar(rstd0[:], mv0[:, :, 1], EPS, 1.0, ALU.add, ALU.mult))
                    pool.tensor_tensor(rstd0[:], rstd0[:], half[:, 0:4], ALU.pow).then_inc(rstd0_done, 1)
                if what == "low0":
                    pool.wait_ge(xh_done, t.n + 1)
                    pool.tensor_tensor(chunk(keep["xl"], t), h2[:], chunk(keep["xh"], t).bitcast(F32),
                                       ALU.subtract).then_inc(xl_done, 1)
                if what == "low1":
                    pool.wait_ge(xTh_done, t.n + 1)
                    pool.tensor_tensor(chunk(keep["xl"], t), xT[:], chunk(keep["xh"], t).bitcast(F32),
                                       ALU.subtract).then_inc(xTl_done, 1)
                if what == "post0":
                    pool.wait_ge(var_done, t.n + 1)
                    settle(pool, passed_pool)
                    c = Tally(pool, pool1, 1, t.n)
                    c.link(pool.tensor_scalar(rstd[:], mv[:, :, 1], EPS, 1.0, ALU.add, ALU.mult))
                    pool.tensor_tensor(rstd[:], rstd[:], half[:, 0:4], ALU.pow).then_inc(rstd_done, 1)
                if what == "norm" and out is None:
                    pool.wait_ge(xn_done, t.n + 1)
                    settle(pool, passed_pool)
                    pool.tensor_copy(keep["xa"][:, ds(t.n * 4, 4), :], xn[:]).then_inc(xa_done, 1)

            skewed(pool, NC_, parts_of(step))

        @block.scalar
        def _(act):
            act.wait_ge(loaded, 16 * len(loads))

            def step(what, t, k, fs):
                if what == "pre" and norm_first:
                    act.wait_ge(qb_full, t.n + 1)
                    if not t.first:
                        act.wait_ge(xl_done, t.n)
                    act.activation(h2[:], QB[:], ACT.Identity, scale=cols[:, 0:1],
                                   bias=cols[:, 1:2]).then_inc(qb_free, 1)
                    act.wait_ge(qb_free, t.n + 1)
                    act.activation(chunk(keep["xh"], t), h2[:], ACT.Copy).then_inc(xh_done, 1)
                if what == "hidden":
                    j, q = t.n * E_ + k, par(t, k)
                    new = isinstance(j, int) and j < ago
                    for f in fs:
                        act.wait_ge(h_full, j * 4 + f + 1)
                        if f == 0 and not new:
                            act.wait_ge(lo_done, (j - ago) * 2 + 2)
                        act.activation(hf[:, q, f], HB[:, f], gelu,
                                       bias=b1[:, k * FB + f:k * FB + f + 1]).then_inc(h_free, 1)
                        if f % 2:
                            act.wait_ge(h_free, j * 4 + f + 1)
                            if f == 1 and not new:
                                act.wait_ge(y_full, j - ago + 1)
                            act.activation(hh[:, q, f - 1:f + 1], hf[:, q, f - 1:f + 1],
                                           ACT.Copy).then_inc(hi_done, 1)
                if what == "down" and norm_first and fs[-1] == FB - 1:
                    act.wait_ge(y_full, t.n + 1)
                    act.activation(acc[:, t.p], YB[:, 0], ACT.Identity, bias=cols[:, 2:3]).then_inc(y_free, 1)
                if what == "post1":
                    act.wait_ge(pb_full, t.n * jobs + 2)
                    if not t.first:
                        act.wait_ge(xTl_done, t.n)
                        act.wait_ge(pb_full, t.n * jobs)
                    act.activation(xT[:], PB[:], ACT.Copy).then_inc(pb_free, 1)
                    act.wait_ge(pb_free, t.n * jobs + 2)
                    act.activation(chunk(keep["xh"], t), xT[:], ACT.Copy).then_inc(xTh_done, 1)

            skewed(act, NC_, parts_of(step))

        @block.vector
        def _(dve):

            def step(what, t, k, fs):
                x1 = lambda a: keep["x1"][:, ds(t.n * 4 + a, 1), :].rearrange("p a c -> p (a c)")
                if what == "stats":
                    c = Tally(dve, ln0, 11, t.n)
                    for a in range(4):
                        c.inc(dve.bn_stats(st0[:, a, :], x1(a)))
                    c.wait()
                    settle(dve, passed_dve)
                    for a in range(4):
                        ins = dve.bn_aggr(mv0[:, a, :], st0[:, a, :])
                        ins.then_inc(var0_done, 1) if a == 3 else c.inc(ins)
                if what == "pre" and norm_first:
                    if not t.first:
                        dve.wait_ge(qb_full, t.n)
                    dve.wait_ge(rstd0_done, t.n + 1)
                    c = Tally(dve, ln0, 11, t.n)
                    c.n = 7
                    for a in range(4):
                        c.inc(dve.tensor_scalar(hn[:, a, :], x1(a), mv0[:, a, 0:1], rstd0[:, a:a + 1],
                                                ALU.subtract, ALU.mult))
                if what == "hidden":
                    j, q = t.n * E_ + k, par(t, k)
                    for f in fs[::2]:
                        dve.wait_ge(hi_done, j * 2 + f // 2 + 1)
                        if f == 0 and not (isinstance(j, int) and j < ago):
                            dve.wait_ge(y_full, j - ago + 1)
                        dve.tensor_tensor(hl[:, q, f:f + 2], hf[:, q, f:f + 2], hh[:, q, f:f + 2].bitcast(F32),
                                          ALU.subtract).then_inc(lo_done, 1)
                if what == "down" and not norm_first:
                    j, q = t.n * E_ + k, par(t, k)
                    dve.wait_ge(y_full, j + 1)
                    c = Tally(dve, comb, E_ - 2, t.n)
                    c.n = k - 1
                    if k == 0:
                        dve.wait_ge(g_in[t.p], (t.half + 1) * 32)
                        dve.tensor_tensor(acc[:, t.p], YB[:, q], G[t.p][:, k], ALU.mult).then_inc(y_free, 1)
                        dve.wait_ge(y_free, j + 1)
                        dve.wait_ge(qb_full, t.n + 1)
                        dve.tensor_tensor(acc[:, t.p], acc[:, t.p], QB[:], ALU.add).then_inc(qb_free, 1)
                        dve.wait_ge(qb_free, t.n + 1)
                    else:
                        dve.tensor_tensor(tmp[:], YB[:, q], G[t.p][:, k], ALU.mult).then_inc(y_free, 1)
                        dve.wait_ge(y_free, j + 1)
                        ins = dve.tensor_tensor(acc[:, t.p], acc[:, t.p], tmp[:], ALU.add)
                        if k < E_ - 1:
                            c.link(ins)
                        else:
                            ins.then_inc(acc_done, 1)
                if what == "post0":
                    dve.wait_ge(pb_full, t.n * jobs + 1)
                    res = keep["xs" if norm_first else "xa"]
                    if not t.first:
                        if out is None:
                            dve.wait_ge(xa_done, t.n)
                        else:
                            dve.wait_ge(stored, t.n * 16)
                    dve.tensor_tensor(r[:], PB[:].rearrange("p (a c) -> p a c", a=4),
                                      res[:, ds(t.n * 4, 4), :], ALU.add).then_inc(pb_free, 1)
                    dve.wait_ge(pb_free, t.n * jobs + 1)
                    c = Tally(dve, ln1, 10, t.n)
                    for a in range(4):
                        c.inc(dve.bn_stats(st[:, a, :], r[:, a, :]))
                    c.wait()
                    settle(dve, passed_dve)
                    for a in range(4):
                        ins = dve.bn_aggr(mv[:, a, :], st[:, a, :])
                        ins.then_inc(var_done, 1) if a == 3 else c.inc(ins)
                if what == "norm":
                    c = Tally(dve, ln1, 10, t.n)
                    c.n = 7
                    if transposed and not t.first:
                        dve.wait_ge(pb_full, t.n * jobs)
                    dve.wait_ge(rstd_done, t.n + 1)
                    for a in range(4):
                        ins = dve.tensor_scalar(xn[:, a, :], r[:, a, :], mv[:, a, 0:1], rstd[:, a:a + 1],
                                                ALU.subtract, ALU.mult)
                        ins.then_inc(xn_done, 1) if a == 3 else c.inc(ins)
                if what == "post2":
                    dve.wait_ge(pb_full, t.n * jobs + 3)
                    dve.tensor_copy(keep["logits"][:, ds(t.n * 4, 4), :],
                                    PB[:, 0:4 * E].rearrange("p (a e) -> p a e", a=4)).then_inc(pb_free, 1)

            skewed(dve, NC_, parts_of(step))

        @block.tensor
        def _(pe):

            def split_product(dst, wh, wl, xh, xl, first, last):
                pe.matmul(dst, wh, xh, start=first, stop=False)
                pe.matmul(dst, wh, xl, start=False, stop=False)
                return pe.matmul(dst, wl, xh, start=False, stop=last)

            def step(what, t, k, fs):
                if what == "pre" and norm_first:
                    pe.wait_ge(ln0, (t.n + 1) * 11)
                    if not t.first:
                        pe.wait_ge(qb_free, t.n)
                    for a in range(4):
                        ins = pe.transpose(QB[:, a * P:(a + 1) * P], hn[:, a, :], keep["ident"][:])
                    ins.then_inc(qb_full, 1)
                if what == "hidden":
                    j = t.n * E_ + k
                    if fs[0] == 0 and norm_first:
                        pe.wait_ge(xh_done, t.n + 1)
                        pe.wait_ge(xl_done, t.n + 1)
                    for f in fs:
                        if not (isinstance(j, int) and j < 1):
                            pe.wait_ge(h_free, j * 4 + f - 3)
                        s = slice((k * FB + f) * P, (k * FB + f + 1) * P)
                        split_product(HB[:, f], keep["w1h"][:, s], keep["w1l"][:, s], chunk(keep["xh"], t),
                                      chunk(keep["xl"], t), True, True).then_inc(h_full, 1)
                if what == "down":
                    j, q = t.n * E_ + k, par(t, k)
                    if fs[0] == 0 and not (isinstance(j, int) and j < ago):
                        pe.wait_ge(y_free, j - ago + 1)
                    for f in fs:
                        if f % 2 == 0:
                            pe.wait_ge(lo_done, j * 2 + f // 2 + 1)
                        s = slice((k * FB + f) * P, (k * FB + f + 1) * P)
                        ins = split_product(YB[:, q], keep["w2h"][:, s], keep["w2l"][:, s], hh[:, q, f],
                                            hl[:, q, f], f == 0, f == FB - 1)
                    if fs[-1] == FB - 1:
                        ins.then_inc(y_full, 1)
                    if k == 0 and not norm_first:
                        pe.wait_ge(loaded, 16 * len(loads))
                        pe.wait_ge(g_in[t.p], (t.half + 1) * 32)
                        if not t.first:
                            pe.wait_ge(qb_free, t.n)
                        pe.matmul(QB[:], b2[:], g8[t.p][:], start=True, stop=True).then_inc(qb_full, 1)
                if what == "post0":
                    if norm_first:
                        pe.wait_ge(y_free, t.n + 1)
                    else:
                        pe.wait_ge(acc_done, t.n + 1)
                    if not t.first:
                        pe.wait_ge(pb_free, t.n * jobs)
                    for a in range(4):
                        ins = pe.transpose(PB[:, a * P:(a + 1) * P], acc[:, t.p, a * P:(a + 1) * P],
                                           keep["ident"][:])
                    ins.then_inc(pb_full, 1)
                if what == "post1":
                    pe.wait_ge(xn_done, t.n + 1)
                    pe.wait_ge(pb_free, t.n * jobs + 1)
                    for a in range(4):
                        ins = pe.transpose(PB[:, a * P:(a + 1) * P], xn[:, a, :], keep["ident"][:])
                    ins.then_inc(pb_full, 1)
                if what == "post2":
                    pe.wait_ge(pb_free, t.n * jobs + 2)
                    for a in range(4):
                        ins = pe.matmul(PB[:, a * E:(a + 1) * E], xT[:, a * P:(a + 1) * P],
                                        keep["gate0"][:], start=True, stop=True)
                    ins.then_inc(pb_full, 1)

            skewed(pe, NC_, parts_of(step))


def threshold(nc, keep, gates_dram, w1, w2):
    with ExitStack() as ctx:
        m = Mem(nc, ctx, "t")
        N = NT * E
        L = keep["logits"][:].rearrange("p a e -> p (a e)")
        Ls = m.sb("Ls", [P, N])
        below = m.sb("below", [P, 3, N])
        ones = m.sb("ones", [P, P])
        cnt = m.sb("cnt", [P, 3])
        neg = m.sb("neg", [P, 1])
        sign = m.sb("sign", [P, 1])
        rank = m.sb("rank", [P, 1])
        bits = m.sb("bits", [P, 3])
        bit = m.sb("bit", [P, 1])
        bits_u = m.sb("bits_u", [P, 3], U32)
        found = m.sb("found", [P, 1], U32)
        cand = m.sb("cand", [P, 3], U32)
        fits = m.sb("fits", [P, 3])
        taken = m.sb("taken", [P, 1])
        add = m.sb("add", [P, 1], U32)
        kth = m.sb("kth", [P, 1])
        gt = m.sb("gt", [P, N])
        gT = m.sb("gT", [P, 2, P])
        CP = m.ps("CP", [P, 512])
        TP = m.ps("TP", [P, 512])
        split = Split(m, keep, w1, w2)
        own = m.sem("own")
        counted, summed = m.sem("counted"), m.sem("summed")
        turned, copied, sent = m.sem("turned"), m.sem("copied"), m.sem("sent")
        block = ctx.enter_context(nc.Block())
        TURNS, EACH = 5, 3
        PAIRS = TURNS * EACH

        @block.vector
        def _(dve):
            t = Tally(dve, own, 0, 0)
            dve.memset(ones[:], 1.0)
            for k in range(3):
                dve.memset(bits[:, k:k + 1], float((k + 1) * 2 ** 29))
            t.link(dve.memset(found[:], 0))
            t.link(dve.tensor_copy(bits_u[:], bits[:]))
            dve.tensor_scalar(below[:, 0], L, 0.0, None, ALU.is_lt, ALU.add, accum_out=cnt[:, 0:1]).then_inc(counted, 1)
            dve.wait_ge(summed, 1)
            t.link(dve.tensor_scalar(neg[:], CP[:, 0:1], float(KEEP_FROM), None, ALU.is_ge))
            t.link(dve.tensor_scalar(sign[:], neg[:], -2.0, 1.0, ALU.mult, ALU.add))
            t.link(dve.tensor_scalar(rank[:], neg[:], float(T * E - 2 * KEEP_FROM + 1), float(KEEP_FROM - 1),
                                     ALU.mult, ALU.add))
            t.link(dve.tensor_scalar(Ls[:], L, sign[:], None, ALU.mult))

            def count(n):
                for k in range(n):
                    ins = dve.tensor_scalar(below[:, k], Ls[:], cand[:, k:k + 1].bitcast(F32), None, ALU.is_lt,
                                            ALU.add, accum_out=cnt[:, k:k + 1])
                ins.then_inc(counted, 1)

            first = t.n
            with dve.Fori(0, TURNS) as i:
                t = Tally(dve, own, 7 * EACH, i)
                t.n = first
                for u in range(EACH):
                    t.link(dve.tensor_tensor(cand[:], found[:].to_broadcast([P, 3]), bits_u[:], ALU.bitwise_or))
                    count(3)
                    t.link(dve.tensor_copy(bit[:], bits[:, 0:1]))
                    t.link(dve.tensor_scalar(bits[:], bits[:], 0.25, None, ALU.mult))
                    t.link(dve.tensor_copy(bits_u[:], bits[:]))
                    dve.wait_ge(summed, i * EACH + u + 2)
                    t.link(dve.tensor_scalar(fits[:], CP[:, 0:3], rank[:], None, ALU.is_le, ALU.add,
                                             accum_out=taken[:]))
                    t.link(dve.tensor_scalar(add[:], taken[:], bit[:], None, ALU.mult))
                    t.link(dve.tensor_tensor(found[:], found[:], add[:], ALU.bitwise_or))
            t = Tally(dve, own, 0, 0)
            t.n = first + 7 * PAIRS
            t.link(dve.tensor_scalar(cand[:, 0:1], found[:], 1, None, ALU.bitwise_or))
            count(1)
            dve.wait_ge(summed, PAIRS + 2)
            t.link(dve.tensor_scalar(add[:], CP[:, 0:1], rank[:], None, ALU.is_le))
            t.link(dve.tensor_tensor(found[:], found[:], add[:], ALU.bitwise_or))
            t.link(dve.tensor_tensor(kth[:], found[:].bitcast(F32), sign[:], ALU.mult))
            Let = L.rearrange("p (t e) -> p e t", e=E)
            dve.scalar_tensor_tensor(out=gt[:].rearrange("p (e t) -> p e t", e=E), in0=Let, scalar=kth[:],
                                     in1=Let, op0=ALU.is_ge, op1=ALU.mult).then_inc(counted, 1)
            dve.wait_ge(turned, 1)
            dve.tensor_copy(gT[:].rearrange("p a b -> p (a b)"), TP[:, 0:N]).then_inc(copied, 1)

        @block.tensor
        def _(pe):
            def sum_up(n):
                pe.matmul(CP[:, 0:n], ones[:], cnt[:, 0:n], start=True, stop=True).then_inc(summed, 1)

            pe.wait_ge(counted, 1)
            sum_up(1)
            with pe.Fori(0, TURNS) as i:
                for u in range(EACH):
                    pe.wait_ge(counted, i * EACH + u + 2)
                    sum_up(3)
            pe.wait_ge(counted, PAIRS + 2)
            sum_up(1)
            pe.wait_ge(counted, PAIRS + 3)
            for a in range(2):
                ins = pe.transpose(TP[:, a * P:(a + 1) * P], gt[:, a * P:(a + 1) * P], keep["ident"][:])
            ins.then_inc(turned, 1)

        @block.sync
        def _(sp):
            split.load(sp)
            sp.wait_ge(copied, 1)
            rows = gates_dram.rearrange("e (t j) -> (e t) j", j=P).rearrange("(a p) j -> p a j", p=P)
            sp.dma_start(rows, gT[:]).then_inc(sent, 16)
            sp.wait_ge(sent, 16)

        @block.scalar
        def _(act):
            split.high(act)

        @block.gpsimd
        def _(pool):
            split.low(pool)


ORDER_1 = [("turn", 0), ("fetch", 0), ("mix", 0), ("scores", 0), ("copy", 0), ("norm", 0),
           ("shift", 0), ("scores", 1), ("xT", 0), ("context", 0), ("next", 0), ("project", 0),
           ("weights", 0), ("shift", 1), ("router", 0), ("split", 0), ("wide", 0), ("features", 0),
           ("weights", 1), ("rank", 0), ("linear", 0), ("values", 0), ("back", 0), ("values", 1),
           ("gates", 0), ("queries", 0), ("back", 1), ("qT", 0)]
LH, GH = 4, 12
GW = GH * HD


def attention_1(nc, d, keep, gates, w1, w2):
    with ExitStack() as ctx:
        m = Mem(nc, ctx, "b")
        (b32, f32), (b16, f16), (bbf, bf16) = (unpacked(m, n) for n in ("b32", "b16", "bbf"))
        wql, wkl, wg, wo = f32["wql"], f32["wkl"], f32["wg"], f32["wo"]
        cols = f32["cols"]
        same_head, before, gate1 = f32["same_head"][0:GW], f32["before"], f32["gate1"]
        ident16, identb, causal, causalT = f16["ident16"], bf16["identb"], bf16["causal"], bf16["causalT"]
        bo = m.sb("bo", [P, P])
        xs = [m.sb(f"xs{p}", [P, 2, C]) for p in range(2)]
        xb = [m.sb(f"xb{p}", [P, 2, C]) for p in range(2)]
        xT = m.sb("xT", [P, TB])
        high = m.sb("high", [P, 2, TB], F16)
        qs = [m.sb(f"qs{p}", [P, TB], F16) for p in range(2)]
        ks = [m.sb(f"ks{p}", [P, TB], F16) for p in range(2)]
        va = [m.sb(f"va{p}", [P, 2, LH, 32]) for p in range(2)]
        gv = [m.sb(f"gv{p}", [P, 2, GW + 1]) for p in range(2)]
        kf = [m.sb(f"kf{p}", [P, 2, GW]) for p in range(2)]
        qT = [m.sb(f"qT{p}", [GW, TB]) for p in range(2)]
        qm = m.sb("qm", [P, 2, GH])
        qd = m.sb("qd", [P, 2, GW])
        qe = m.sb("qe", [P, 2, GW])
        qsum = m.sb("qsum", [P, 2, GH])
        qr = m.sb("qr", [P, 2, GH])
        qn = m.sb("qn", [P, 2, GW])
        kn = m.sb("kn", [P, 2, GW])
        ke = m.sb("ke", [P, 2, GW])
        mx = m.sb("mx", [P, 2, LH])
        mpad = m.sb("mpad", [P, 2, LH, 32], F16)
        q2 = m.sb("q2", [P, 2, P], F16)
        pt = m.sb("pt", [P, 2, LH, 2 * P])
        ots = m.sb("ots", [P, 2, P])
        rc = m.sb("rc", [P, 2, LH])
        den = m.sb("den", [GW, 3])
        rinv = m.sb("rinv", [GW, 3])
        ctxn = m.sb("ctxn", [GW, 3, GW])
        ob = [m.sb(f"ob{p}", [P, 2, C]) for p in range(2)]
        aT = m.sb("aT", [P, TB])
        half = m.sb("half", [P, 2])
        r = m.sb("r", [P, 2, C])
        st = m.sb("st", [P, 2, 6])
        mv = m.sb("mv", [P, 2, 2])
        rstd = m.sb("rstd", [P, 2])
        xn = m.sb("xn", [P, 2, C])
        x3T = m.sb("x3T", [P, TB])
        lg = m.sb("lg", [P, 2, E])
        lm = m.sb("lm", [P, 2])
        ld = m.sb("ld", [P, 2, E])
        le = m.sb("le", [P, 2, E])
        gtr = m.sb("gtr", [P, 2, E, E])
        eqr = m.sb("eqr", [P, 2, E, E])
        rank = m.sb("rank", [P, 2, E])
        sel = m.sb("sel", [P, 2, E])
        gsum = m.sb("gsum", [P, 2])
        grec = m.sb("grec", [P, 2])
        gt = m.sb("gt", [P, 2, E])
        gT = m.sb("gT", [2 * E, P])

        share = w1.shape[1] // NB
        stage = m.sb("stage", [P, 2, 2, share])
        split_to = ((w1, keep["w1h"], keep["w1l"]), (w2, keep["w2h"], keep["w2l"]))

        SS = m.ps("SS", [P, 2, 512])
        OT = m.ps("OT", [P, 512])
        MI = m.ps("MI", [P, 512])
        W1 = m.ps("W1", [P, 512])
        WG = m.ps("WG", [P, 2, 512])
        W3 = m.ps("W3", [P, 512])
        MT = MI[:, 0:P // 2].bitcast(F16)

        names = ("loaded cleared copied xb_done w1_full w1_free high_done wg_full wg_free "
                 "feat_own first_heads kn_done keys_done qd_done qe_done qn_done ss_full ss_free mx_own mpad_done "
                 "mi_full mi_free pv_done ot_free norm_own ctx_own w3_full w3_free r_own var_done "
                 "pool_ln rstd_done xn_done xa_done xh_done xl_done lg_own ld_done le_done gt_done sent "
                 "passed_pool passed_dve landed0 landed1 split_high split_low")
        s = {n: m.sem(n) for n in names.split()}
        loads = [(b32[:], d["b32"]), (b16[:], d["b16"]), (bbf[:], d["bbf"]), (bo[:], d["b_bo"].to_broadcast([P, C]))]
        scale = float(HD) ** -0.5

        def ready(eng):
            eng.wait_ge(s["loaded"], 16 * len(loads))
            eng.wait_ge(s["cleared"], 3)

        ahead = ("fetch", "copy", "xT", "project", "wide", "features", "queries", "qT")
        behind = ("turn", "mix", "norm", "next", "router", "rank", "gates")

        def parts_of(act):
            def go(pre, main, post):
                for what, k in ORDER_1:
                    t = pre if what in ahead else post if what in behind else main
                    if t:
                        act(what, t, k)
            return go

        block = ctx.enter_context(nc.Block())

        @block.sync
        def _(sp):
            for dst, src in loads:
                sp.dma_start(dst, src).then_inc(s["loaded"], 16)

            def part(what, t, k):
                if what == "fetch":
                    if not t.early:
                        sp.wait_ge(s["split_low"], t.n - 1)
                    for a, (src, _, _) in enumerate(split_to):
                        sp.dma_start(stage[:, t.p, a], src[:, ds(t.n * share, share)]).then_inc(s["landed%d" % t.p], 16)
                if what == "gates":
                    sp.wait_ge(s["w3_free"], t.n * 5 + 5)
                    for a in range(2):
                        sp.dma_start(gates[:, ds(t.n * TB + a * P, P)],
                                     gT[a * E:(a + 1) * E, :]).then_inc(s["sent"], 16)

            skewed(sp, NB, parts_of(part))
            sp.wait_ge(s["sent"], 32 * NB)

        @block.gpsimd
        def _(pool):
            pool.memset(half[:], -0.5)
            for v in va:
                pool.memset(v[:], 0.0)
            for v in ob:
                pool.memset(v[:], 0.0)
            pool.memset(mpad[:], 0.0).then_inc(s["cleared"], 1)
            pool.wait_ge(s["cleared"], 1)
            for a in range(2):
                pool.memset(va[a][:, :, :, HD:HD + 1], 1.0)
                pool.memset(gv[a][:, :, GW:GW + 1], 1.0).then_inc(s["cleared"], 1)
            ready(pool)

            def part(what, t, k):
                if what == "copy":
                    if not t.early:
                        pool.wait_ge(s["w1_full"], (t.n - 2) * 3 + 1)
                        pool.wait_ge(s["xn_done"], t.n - 1)
                    settle(pool, s["passed_pool"])
                    pool.tensor_copy(xs[t.p][:], keep["xa"][:, ds(t.n * 2, 2), :]).then_inc(s["copied"], 1)
                    pool.wait_ge(s["copied"], t.n + 1)
                    for a in range(2):
                        ins = pool.tensor_tensor(xb[t.p][:, a, :], xs[t.p][:, a, :], bo[:], ALU.add)
                    ins.then_inc(s["xb_done"], 1)
                if what == "split":
                    pool.wait_ge(s["split_high"], t.n + 1)
                    for a, (_, w_high, w_low) in enumerate(split_to):
                        cut = ds(t.n * share, share)
                        ins = pool.tensor_tensor(w_low[:, cut], stage[:, t.p, a], w_high[:, cut].bitcast(F32),
                                                 ALU.subtract)
                    ins.then_inc(s["split_low"], 1)
                if what == "mix":
                    pool.wait_ge(s["var_done"], t.n + 1)
                    settle(pool, s["passed_pool"])
                    c = Tally(pool, s["pool_ln"], 1, t.n)
                    c.link(pool.tensor_scalar(rstd[:], mv[:, :, 1], EPS, 1.0, ALU.add, ALU.mult))
                    pool.tensor_tensor(rstd[:], rstd[:], half[:], ALU.pow).then_inc(s["rstd_done"], 1)
                if what == "next":
                    pool.wait_ge(s["xh_done"], t.n + 1)
                    xh = keep["xh"][:, ds(t.n * TB, TB)]
                    pool.tensor_tensor(keep["xl"][:, ds(t.n * TB, TB)], x3T[:], xh.bitcast(F32),
                                       ALU.subtract).then_inc(s["xl_done"], 1)
                if what == "norm":
                    pool.wait_ge(s["xn_done"], t.n + 1)
                    settle(pool, s["passed_pool"])
                    pool.tensor_copy(keep["xa"][:, ds(t.n * 2, 2), :], xn[:]).then_inc(s["xa_done"], 1)

            skewed(pool, NB, parts_of(part))

        @block.scalar
        def _(act):
            ready(act)

            def part(what, t, k):
                if what == "xT":
                    act.wait_ge(s["w1_full"], t.n * 3 + 1)
                    if not t.first:
                        act.wait_ge(s["wg_full"], t.n)
                    act.activation(xT[:], W1[:, 0:TB], ACT.Copy).then_inc(s["w1_free"], 1)
                if what == "project":
                    act.wait_ge(s["w1_full"], t.n * 3 + 2)
                    if not t.first:
                        act.wait_ge(s["w1_free"], t.n * 3 - 1)
                    act.activation(high[:, 0], W1[:, 0:TB], ACT.Copy)
                    act.activation(high[:, 1], W1[:, TB:2 * TB], ACT.Identity,
                                   bias=cols[:, 0:1]).then_inc(s["high_done"], 1)
                if what == "features":
                    v = WG[:, :, 2 * GW:2 * GW + C]
                    act.wait_ge(s["kn_done"], t.n + 1)
                    if not t.first:
                        act.wait_ge(s["wg_free"], t.n)
                    act.activation(ke[:], kn[:], ACT.Exp)
                    act.wait_ge(s["qd_done"], t.n + 1)
                    if not t.early:
                        act.wait_ge(s["mi_full"], (t.n - 1) * 6)
                    act.activation(gv[t.p][:, :, 0:GW], v[:, :, LH * HD:], ACT.Copy)
                    act.activation(va[t.p][:, :, :, 0:HD],
                                   v[:, :, 0:LH * HD].rearrange("p a (h e) -> p a h e", e=HD),
                                   ACT.Copy).then_inc(s["keys_done"], 1)
                    act.activation(qe[:], qd[:], ACT.Exp).then_inc(s["qe_done"], 1)
                if what == "qT":
                    act.wait_ge(s["w1_full"], t.n * 3 + 3)
                    if not t.early:
                        act.wait_ge(s["mi_full"], (t.n - 2) * 6 + 4)
                    act.activation(qT[t.p][:], W1[0:GW, 0:TB], ACT.Copy).then_inc(s["w1_free"], 1)
                if what == "weights":
                    act.wait_ge(s["ss_full"], t.n * 4 + 3 + k)
                    if not t.first:
                        act.wait_ge(s["pv_done"], t.n * 2 - 1 + k)
                    n = P * (k + 1)
                    act.activation(pt[:, k, :, 0:n],
                                   SS[:].rearrange("p b (h j) -> p (b h) j", h=2)[:, :, 0:n],
                                   ACT.Exp, scale=scale).then_inc(s["ss_free"], 1)
                if what == "linear":
                    act.wait_ge(s["mi_full"], t.n * 6 + 4)
                    act.activation(ob[t.p][BK:P, 0, LH * HD:], MI[BK:P, 0:GW], ACT.Copy)
                    act.activation(ob[t.p][:, 1, LH * HD:], MI[:, GW:2 * GW], ACT.Copy).then_inc(s["mi_free"], 1)
                if what == "back":
                    act.wait_ge(s["pv_done"], t.n * 2 + k + 1)
                    if not t.first:
                        act.wait_ge(s["mi_full"], t.n * 6 - 1 + k)
                    act.activation(ots[:, k], OT[:, k * P:(k + 1) * P], ACT.Copy).then_inc(s["ot_free"], 1)
                if what == "split":
                    act.wait_ge(s["landed%d" % t.p], 32 * (t.half + 1))
                    for a, (_, w_high, _) in enumerate(split_to):
                        ins = act.activation(w_high[:, ds(t.n * share, share)], stage[:, t.p, a], ACT.Copy)
                    ins.then_inc(s["split_high"], 1)
                if what == "turn":
                    act.wait_ge(s["w3_full"], t.n * 5 + 1)
                    act.activation(aT[:], W3[:, 0:TB], ACT.Copy).then_inc(s["w3_free"], 1)
                if what == "next":
                    act.wait_ge(s["w3_full"], t.n * 5 + 3)
                    if not t.first:
                        act.wait_ge(s["xl_done"], t.n)
                    act.activation(x3T[:], W3[:, 0:TB], ACT.Copy).then_inc(s["w3_free"], 1)
                    act.wait_ge(s["w3_free"], t.n * 5 + 3)
                    act.activation(keep["xh"][:, ds(t.n * TB, TB)], x3T[:], ACT.Copy).then_inc(s["xh_done"], 1)
                if what == "router":
                    act.wait_ge(s["ld_done"], t.n + 1)
                    act.activation(le[:], ld[:], ACT.Exp).then_inc(s["le_done"], 1)
                if what == "gates":
                    act.wait_ge(s["w3_full"], t.n * 5 + 5)
                    if not t.first:
                        act.wait_ge(s["sent"], t.n * 32)
                    act.activation(gT[:], W3[0:2 * E, 0:P], ACT.Copy).then_inc(s["w3_free"], 1)

            skewed(act, NB, parts_of(part))

        @block.vector
        def _(dve):
            ready(dve)
            heads = lambda v: v.rearrange("p a (h e) -> p a h e", e=HD)

            def part(what, t, k):
                if what == "project":
                    dve.wait_ge(s["high_done"], t.n + 1)
                    if not t.early:
                        dve.wait_ge(s["ss_full"], (t.n - 1) * 4)
                    for out, a in ((qs[t.p], 0), (ks[t.p], 1)):
                        ins = dve.scalar_tensor_tensor(out=out[:], in0=high[:, a], scalar=cols[:, 1 + a:2 + a],
                                                       in1=W1[:, a * TB:(a + 1) * TB], op0=ALU.mult, op1=ALU.add)
                    ins.then_inc(s["w1_free"], 1)
                if what == "features":
                    q, kk = WG[:, :, 0:GW], WG[:, :, GW:2 * GW]
                    dve.wait_ge(s["wg_full"], t.n + 1)
                    if not t.early:
                        dve.wait_ge(s["mi_full"], (t.n - 1) * 6)
                    c = Tally(dve, s["feat_own"], 3, t.n)
                    dve.tensor_scalar(kn[:], kk, 0.0, None, ALU.min).then_inc(s["kn_done"], 1)
                    c.link(dve.tensor_reduce(qm[:], heads(q), AX.X, ALU.max))
                    dve.tensor_tensor(heads(qd[:]), heads(q), qm[:, :, :, None].to_broadcast([P, 2, GH, HD]),
                                      ALU.subtract).then_inc(s["qd_done"], 1)
                    dve.wait_ge(s["keys_done"], t.n + 1)
                    dve.scalar_tensor_tensor(out=kf[t.p][:], in0=kk, scalar=0.0, in1=ke[:], op0=ALU.max,
                                             op1=ALU.add).then_inc(s["wg_free"], 1)
                if what == "queries":
                    c = Tally(dve, s["feat_own"], 3, t.n)
                    c.n = 1
                    dve.wait_ge(s["qe_done"], t.n + 1)
                    c.link(dve.tensor_reduce(qsum[:], heads(qe[:]), AX.X, ALU.add))
                    c.link(dve.reciprocal(qr[:], qsum[:]))
                    if not t.first:
                        dve.wait_ge(s["w1_full"], t.n * 3)
                    dve.tensor_tensor(heads(qn[:]), heads(qe[:]), qr[:, :, :, None].to_broadcast([P, 2, GH, HD]),
                                      ALU.mult).then_inc(s["qn_done"], 1)
                if what == "scores":
                    dve.wait_ge(s["ss_full"], t.n * 4 + k + 1)
                    c = Tally(dve, s["mx_own"], 2, t.n)
                    c.n = k
                    dve.tensor_reduce(mx[:, k], SS[:].rearrange("p b (h j) -> p (b h) j", h=2)[:, :, 0:P * (k + 1)],
                                      AX.X, ALU.max).then_inc(s["ss_free"], 1)
                    dve.wait_ge(s["ss_free"], t.n * 4 + k + 1)
                    if not t.first:
                        dve.wait_ge(s["mi_full"], t.n * 6 - 5 + 2 * k)
                    c.link(dve.tensor_copy(mpad[:, k, :, 24], mx[:, k]))
                    dve.tensor_tensor(mpad[:, k, :, 25], mx[:, k], mpad[:, k, :, 24],
                                      ALU.subtract).then_inc(s["mpad_done"], 1)
                if what == "shift":
                    dve.wait_ge(s["mi_full"], t.n * 6 + 2 * k + 1)
                    if not t.first:
                        dve.wait_ge(s["ss_full"], t.n * 4 - 1 + k)
                    dve.tensor_tensor(q2[:, k], qs[t.p][:, k * P:(k + 1) * P], MT,
                                      ALU.subtract).then_inc(s["mi_free"], 1)
                if what == "context":
                    cx = MI[0:GW, 0:3 * (GW + 1)].rearrange("p (u e) -> p u e", u=3)
                    dve.wait_ge(s["mi_full"], t.n * 6 + 2)
                    c = Tally(dve, s["ctx_own"], 2, t.n)
                    c.link(dve.tensor_scalar(den[:], cx[:, :, GW], 1e-6, None, ALU.add))
                    c.link(dve.reciprocal(rinv[:], den[:]))
                    if not t.first:
                        dve.wait_ge(s["mi_full"], t.n * 6 - 2)
                    for u in range(3):
                        ins = dve.scalar_tensor_tensor(out=ctxn[:, u], in0=cx[:, u, 0:GW], scalar=rinv[:, u:u + 1],
                                                       in1=same_head[:], op0=ALU.mult, op1=ALU.mult)
                    ins.then_inc(s["mi_free"], 1)
                if what == "back":
                    o4 = MI[:, 0:P].rearrange("p (h e) -> p h e", e=32)
                    dve.wait_ge(s["mi_full"], t.n * 6 + 5 + k)
                    c = Tally(dve, s["norm_own"], 2, t.n)
                    c.n = k
                    c.link(dve.reciprocal(rc[:, k, :], o4[:, :, HD]))
                    dve.tensor_tensor(ob[t.p][:, k, 0:LH * HD].rearrange("p (h e) -> p h e", e=HD),
                                      o4[:, :, 0:HD], rc[:, k, :, None].to_broadcast([P, LH, HD]),
                                      ALU.mult).then_inc(s["mi_free"], 1)
                if what == "mix":
                    dve.wait_ge(s["w3_full"], t.n * 5 + 2)
                    dve.wait_ge(s["xb_done"], t.n + 1)
                    dve.tensor_tensor(r[:], W3[:, 0:TB].rearrange("p (a c) -> p a c", a=2), xb[t.p][:],
                                      ALU.add).then_inc(s["w3_free"], 1)
                    dve.wait_ge(s["w3_free"], t.n * 5 + 2)
                    c = Tally(dve, s["r_own"], 3, t.n)
                    for a in range(2):
                        c.inc(dve.bn_stats(st[:, a, :], r[:, a, :]))
                    c.wait()
                    settle(dve, s["passed_dve"])
                    c.inc(dve.bn_aggr(mv[:, 0, :], st[:, 0, :]))
                    dve.bn_aggr(mv[:, 1, :], st[:, 1, :]).then_inc(s["var_done"], 1)
                if what == "norm":
                    if not t.first:
                        dve.wait_ge(s["xa_done"], t.n)
                        dve.wait_ge(s["w3_full"], t.n * 5)
                    dve.wait_ge(s["rstd_done"], t.n + 1)
                    for a in range(2):
                        ins = dve.tensor_scalar(xn[:, a, :], r[:, a, :], mv[:, a, 0:1], rstd[:, a:a + 1],
                                                ALU.subtract, ALU.mult)
                    ins.then_inc(s["xn_done"], 1)
                if what == "router":
                    dve.wait_ge(s["w3_full"], t.n * 5 + 4)
                    c = Tally(dve, s["lg_own"], 9, t.n)
                    dve.tensor_copy(lg[:], W3[:, 0:2 * E].rearrange("p (a e) -> p a e", a=2)).then_inc(s["w3_free"], 1)
                    dve.wait_ge(s["w3_free"], t.n * 5 + 4)
                    c.link(dve.tensor_reduce(lm[:], lg[:], AX.X, ALU.max))
                    dve.tensor_tensor(ld[:], lg[:], lm[:, :, None].to_broadcast([P, 2, E]),
                                      ALU.subtract).then_inc(s["ld_done"], 1)
                if what == "rank":
                    c = Tally(dve, s["lg_own"], 9, t.n)
                    c.n = 1
                    other = lg[:, :, None, :].to_broadcast([P, 2, E, E])
                    own = lg[:, :, :, None].to_broadcast([P, 2, E, E])
                    c.inc(dve.tensor_tensor(gtr[:], other, own, ALU.is_gt))
                    c.link(dve.tensor_tensor(eqr[:], other, own, ALU.is_equal))
                    c.link(dve.tensor_tensor(eqr[:], eqr[:], before[:, None, :, :].to_broadcast([P, 2, E, E]),
                                             ALU.mult))
                    c.link(dve.tensor_tensor(gtr[:], gtr[:], eqr[:], ALU.add))
                    c.link(dve.tensor_reduce(rank[:], gtr[:], AX.X, ALU.add))
                    dve.wait_ge(s["le_done"], t.n + 1)
                    c.link(dve.scalar_tensor_tensor(out=sel[:], in0=rank[:], scalar=2.0, in1=le[:],
                                                    op0=ALU.is_lt, op1=ALU.mult))
                    c.link(dve.tensor_reduce(gsum[:], sel[:], AX.X, ALU.add))
                if what == "gates":
                    c = Tally(dve, s["lg_own"], 9, t.n)
                    c.n = 8
                    c.link(dve.reciprocal(grec[:], gsum[:]))
                    if not t.first:
                        dve.wait_ge(s["w3_full"], t.n * 5)
                    dve.tensor_tensor(gt[:], sel[:], grec[:, :, None].to_broadcast([P, 2, E]),
                                      ALU.mult).then_inc(s["gt_done"], 1)

            skewed(dve, NB, parts_of(part))

        @block.tensor
        def _(pe):
            ready(pe)

            def job(full, free, per, t, k):
                if not (t.first and k == 0):
                    pe.wait_ge(s[free], t.n * per + k)
                return lambda ins: ins.then_inc(s[full], 1)

            def heads_in_turn(product, mask, n, count):
                for hb in range(2):
                    if hb:
                        ins.then_inc(s["first_heads"], 1)
                        pe.wait_ge(s["first_heads"], count)
                    for b in range(2):
                        product(2 * b + hb, SS[:, b, hb * 2 * P:hb * 2 * P + n], hb == 0)
                    for b in range(2):
                        ins = pe.matmul(SS[:, b, hb * 2 * P:hb * 2 * P + n], identb[:], mask, start=False,
                                        stop=(hb == 1), skip_group_check=True)
                return ins

            def part(what, t, k):
                if what == "xT":
                    done = job("w1_full", "w1_free", 3, t, 0)
                    pe.wait_ge(s["copied"], t.n + 1)
                    for a in range(2):
                        ins = pe.transpose(W1[:, a * P:(a + 1) * P], xs[t.p][:, a, :], keep["ident"][:])
                    done(ins)
                if what == "project":
                    done = job("w1_full", "w1_free", 3, t, 1)
                    pe.matmul(W1[:, 0:TB], wql[:], xT[:], start=True, stop=True)
                    done(pe.matmul(W1[:, TB:2 * TB], wkl[:], xT[:], start=True, stop=True))
                if what == "wide":
                    done = job("wg_full", "wg_free", 1, t, 0)
                    for a in range(2):
                        ins = pe.matmul(WG[:, a, 0:2 * GW + C], xT[:, a * P:(a + 1) * P], wg[:],
                                        start=True, stop=True)
                    done(ins)
                if what == "qT":
                    done = job("w1_full", "w1_free", 3, t, 2)
                    pe.wait_ge(s["qn_done"], t.n + 1)
                    for a in range(2):
                        ins = pe.transpose(W1[0:GW, a * P:(a + 1) * P], qn[:, a, :], keep["ident"][:])
                    done(ins)
                if what == "scores":
                    pe.wait_ge(s["w1_free"], t.n * 3 + 2)
                    done = job("ss_full", "ss_free", 4, t, k)
                    n = P * (k + 1)

                    def product(g, dst, first):
                        rows = slice(32 * g, 32 * g + 32)
                        pe.matmul(dst, qs[t.p][rows, k * P:(k + 1) * P], ks[t.p][rows, 0:n], start=first,
                                  stop=False, skip_group_check=True)

                    done(heads_in_turn(product, causal[:, 1 - k:2, :], n, t.n * 4 + k + 1))
                if what == "shift":
                    done = job("mi_full", "mi_free", 6, t, 2 * k)
                    pe.wait_ge(s["mpad_done"], t.n * 2 + k + 1)
                    done(pe.transpose(MT, mpad[:, k].rearrange("p g r -> p (g r)"), ident16[:]))
                if what == "weights":
                    pe.wait_ge(s["mi_free"], t.n * 6 + 2 * k + 1)
                    done = job("ss_full", "ss_free", 4, t, 2 + k)

                    def product(g, dst, first):
                        rows = slice(32 * g, 32 * g + 32)
                        for w in range(k + 1):
                            pe.matmul(dst[:, w * P:(w + 1) * P], ks[t.p][rows, w * P:(w + 1) * P], q2[rows, k],
                                      start=first and w == 0, stop=False, skip_group_check=True)

                    done(heads_in_turn(product, causalT[:, 1 - k:2, :], P * (k + 1),
                                       t.n * 4 + 3 + k))
                if what == "values":
                    pe.wait_ge(s["ss_free"], t.n * 4 + 3 + k)
                    if k or not t.first:
                        pe.wait_ge(s["ot_free"], t.n * 2 + k)
                    for g in range(LH):
                        for w in range(k + 1):
                            ins = pe.matmul(OT[32 * g:32 * g + 32, k * P:(k + 1) * P], va[t.p][:, w, g, :],
                                            pt[:, k, g, w * P:(w + 1) * P],
                                            start=(w == 0), stop=(w == k))
                    ins.then_inc(s["pv_done"], 1)
                if what == "context":
                    done = job("mi_full", "mi_free", 6, t, 1)
                    pe.wait_ge(s["wg_free"], t.n + 1)
                    n = GW + 1
                    dst = [MI[0:GW, u * n:(u + 1) * n] for u in range(3)]
                    kf_, gv_ = kf[t.p], gv[t.p]
                    pe.matmul(dst[0], kf_[0:BK, 0], gv_[0:BK, 0], start=True, stop=True)
                    pe.matmul(dst[1], kf_[:, 0], gv_[:, 0], start=True, stop=True)
                    pe.matmul(dst[2], kf_[:, 0], gv_[:, 0], start=True, stop=False)
                    done(pe.matmul(dst[2], kf_[0:BK, 1], gv_[0:BK, 1], start=False, stop=True))
                if what == "linear":
                    done = job("mi_full", "mi_free", 6, t, 3)
                    pe.wait_ge(s["w1_free"], t.n * 3 + 3)
                    for b in range(1, 4):
                        a, v = b // 2, b % 2
                        ins = pe.matmul(MI[v * BK:(v + 1) * BK, a * GW:(a + 1) * GW],
                                        qT[t.p][:, b * BK:(b + 1) * BK], ctxn[:, b - 1], start=True, stop=True)
                    done(ins)
                if what == "back":
                    done = job("mi_full", "mi_free", 6, t, 4 + k)
                    pe.wait_ge(s["ot_free"], t.n * 2 + k + 1)
                    done(pe.transpose(MI[:, 0:P], ots[:, k], keep["ident"][:]))
                if what == "turn":
                    done = job("w3_full", "w3_free", 5, t, 0)
                    pe.wait_ge(s["mi_free"], t.n * 6 + 6)
                    for a in range(2):
                        ins = pe.transpose(W3[:, a * P:(a + 1) * P], ob[t.p][:, a, :], keep["ident"][:])
                    done(ins)
                if what == "mix":
                    done = job("w3_full", "w3_free", 5, t, 1)
                    for a in range(2):
                        ins = pe.matmul(W3[:, a * P:(a + 1) * P], aT[:, a * P:(a + 1) * P], wo[:],
                                        start=True, stop=True)
                    done(ins)
                if what == "next":
                    done = job("w3_full", "w3_free", 5, t, 2)
                    pe.wait_ge(s["xn_done"], t.n + 1)
                    for a in range(2):
                        ins = pe.transpose(W3[:, a * P:(a + 1) * P], xn[:, a, :], keep["ident"][:])
                    done(ins)
                if what == "router":
                    done = job("w3_full", "w3_free", 5, t, 3)
                    for a in range(2):
                        ins = pe.matmul(W3[:, a * E:(a + 1) * E], x3T[:, a * P:(a + 1) * P], gate1[:],
                                        start=True, stop=True)
                    done(ins)
                if what == "gates":
                    done = job("w3_full", "w3_free", 5, t, 4)
                    pe.wait_ge(s["gt_done"], t.n + 1)
                    done(pe.transpose(W3[0:2 * E, 0:P], gt[:].rearrange("p a e -> p (a e)"), keep["ident"][:]))

            skewed(pe, NB, parts_of(part))


def program(nc, d, out):
    gates0 = nc.dram_tensor("gates0", [E, T], F32, kind="Internal").ap()
    gates1 = nc.dram_tensor("gates1", [E, T], F32, kind="Internal").ap()
    with ExitStack() as ctx:
        m = Mem(nc, ctx, "keep")
        keep = {"ident": m.sb("ident", [P, P]), "gate0": m.sb("gate0", [P, E]),
                "xh": m.sb("xh", [P, T], F32R), "xl": m.sb("xl", [P, T], F32R),
                "xa": m.sb("xa", [P, NT, C]), "logits": m.sb("logits", [P, NT, E])}
        with ExitStack() as c2:
            m2 = Mem(nc, c2, "early")
            keep["x1"], keep["xs"] = m2.sb("x1", [P, NT, C]), m2.sb("xs", [P, NT, C])
            for n in ("w1h", "w1l", "w2h", "w2l"):
                keep[n] = m2.sb(n, [P, FB * P], F32R)
            attention_0(nc, d, keep, d["m_w1"], d["m_w2"])
            sub = {"b1": d["m_b1"], "cols": d["m_cols"], "b2": d["m_b2"]}
            experts(nc, "m", keep, sub, 1, ACT.Gelu, norm_first=True, transposed=True)
        with ExitStack() as c2:
            m2 = Mem(nc, c2, "late")
            for n in ("w1h", "w1l", "w2h", "w2l"):
                keep[n] = m2.sb(n, [P, E * FB * P], F32R)
            threshold(nc, keep, gates0, d["e0_w1"], d["e0_w2"])
            sub = {"b1": d["e0_b1"], "cols": d["m_cols"], "b2": d["e0_b2"]}
            experts(nc, "e0", keep, sub, E, ACT.Gelu_apprx_tanh, gates=gates0)
            attention_1(nc, d, keep, gates1, d["e1_w1"], d["e1_w2"])
            sub = {"b1": d["e1_b1"], "cols": d["m_cols"], "b2": d["e1_b2"]}
            experts(nc, "e1", keep, sub, E, ACT.Gelu, gates=gates1, out=out)


def heads_to_rows(w, rows, copies=(0, 1, 2)):
    import numpy as np
    lead = w.shape[:-1]
    out = np.zeros(lead + (rows, 4, 32), w.dtype)
    v = w.reshape(lead + (rows, 4, HD))
    for r in copies:
        out[..., HD * r:HD * r + HD] = v
    return out.reshape(lead + (rows, P))


def constants():
    import numpy as np
    bf16 = mybir.dt.np(BF16)
    c = {}
    c["ident"] = np.eye(P, dtype=np.float32)
    c["ident16"] = np.eye(P, dtype=np.float16)
    c["identb"] = np.eye(P, dtype=bf16)
    i, j = np.arange(P)[:, None] % BK, np.arange(P)[None, :]
    mask = np.where((j < BK) | (j - BK <= i), 0.0, NEG)
    c["causal64"] = np.repeat(mask[:, None, :], 4, 1).astype(bf16)
    k = np.zeros((P, 4, BK), np.float16)
    for r in (24, 25):
        k[r::32] = 1.0
    c["kpad"] = k
    i, j = np.arange(P)[:, None], np.arange(P)[None, :]
    z = np.zeros((P, P))
    c["causal128"] = np.stack([z, np.where(j <= i, 0.0, NEG)], 1).astype(bf16)
    c["causal128T"] = np.stack([z, np.where(i <= j, 0.0, NEG)], 1).astype(bf16)
    h = np.arange(GW) // HD
    c["same_head"] = (h[:, None] == h[None, :]).astype(np.float32)
    e = np.arange(E)
    c["before"] = np.ascontiguousarray(np.broadcast_to(e[None, :] < e[:, None], (P, E, E))).astype(np.float32)
    c["spread"] = np.stack([heads_to_rows(c["ident16"], 4, r) for r in ((0, 1), (2,), (0, 2), (1,))], 1)
    low = np.zeros((P, 2), np.float32)
    for g in range(4):
        low[32 * g + 16:32 * g + 24, 0] = -1.0
        low[32 * g + 8:32 * g + 16, 1] = -1.0
    c["low"] = low
    return c


def pack(name, arrays):
    import numpy as np
    return np.concatenate([arrays[part].reshape(P, -1) for part, _ in PACKS[name][1]], 1)


def layout(a):
    import numpy as np
    c = constants()
    out = {"ident": c["ident"], "kpad": c["kpad"]}
    out["x"] = a["L0_attn_x"]
    w, b = a["L0_attn_w_qkv"], a["L0_attn_b_qkv"]
    out["b_out"] = a["L0_attn_b_out"].reshape(1, C)
    ones_rows = np.zeros(P, np.float32)
    ones_rows[24::32] = ones_rows[25::32] = 1.0
    cols = np.stack([a["L0_attn_ln1_g"], a["L0_attn_ln1_b"], b[:C], b[C:2 * C], b[2 * C:], ones_rows], 1)
    own = {"wq": w[:, :C], "wk": w[:, C:2 * C], "wv": w[:, 2 * C:], "wo": a["L0_attn_w_out"], "cols": cols,
           "spread": c["spread"], "ident16": c["ident16"], "identb": c["identb"], "causal": c["causal64"]}
    for name in ("a32", "a16", "abf"):
        out[name] = pack(name, own)
    up = lambda w: np.ascontiguousarray(w.transpose(2, 0, 1).reshape(C, -1))
    down = lambda w: np.ascontiguousarray(w.reshape(-1, FB, P, C).transpose(2, 0, 1, 3).reshape(P, -1))
    per_row = lambda b: np.ascontiguousarray(b.reshape(-1, P).T)
    out["m_w1"] = a["L0_attn_w1"]
    out["m_w2"] = down(a["L0_attn_w2"][None])
    out["m_b1"] = per_row(a["L0_attn_b1"])
    out["m_b2"] = a["L0_attn_b2"].reshape(1, C)
    mc = np.zeros((P, 4), np.float32)
    mc[:, 0], mc[:, 1], mc[:, 2] = a["L0_attn_ln2_g"], a["L0_attn_ln2_b"], a["L0_attn_b2"]
    out["m_cols"] = mc
    out["e0_w1"] = up(a["L0_ffn_w1"])
    out["e0_w2"] = down(a["L0_ffn_w2"].transpose(0, 2, 1))
    out["e0_b1"] = per_row(a["L0_ffn_b1"])
    out["e0_b2"] = a["L0_ffn_b2"]
    out["e1_w1"] = up(a["L1_ffn_w1"].transpose(0, 2, 1))
    out["e1_w2"] = down(a["L1_ffn_w2"])
    out["e1_b1"] = per_row(a["L1_ffn_b1"])
    out["e1_b2"] = a["L1_ffn_b2"]
    wq, wk, wv = a["L1_attn_Wq"], a["L1_attn_Wk"], a["L1_attn_Wv"]
    n = LH * HD
    out["b_bo"] = a["L1_attn_bo"].reshape(1, C)
    bc = np.zeros((P, 4), np.float32)
    bc[:, 0] = ones_rows
    bc[:, 1:3] = c["low"]
    bc[:, 2] += ones_rows
    own = {"wql": heads_to_rows(wq[:, :n], 1)[:, 0], "wkl": heads_to_rows(wk[:, :n], 1)[:, 0],
           "wg": np.concatenate([wq[:, n:], wk[:, n:], wv], 1), "wo": a["L1_attn_Wo"], "cols": bc,
           "same_head": np.pad(c["same_head"], ((0, P - GW), (0, 0))), "before": c["before"],
           "gate1": a["L1_ffn_gate_w"], "ident16": c["ident16"], "identb": c["identb"],
           "causal": c["causal128"], "causalT": c["causal128T"]}
    for name in ("b32", "b16", "bbf"):
        out[name] = pack(name, own)
    out["gate0"] = np.ascontiguousarray(a["L0_ffn_gate_weight"].T)
    return out


def kernel(**inputs):
    import numpy as np
    import concourse.bacc as bacc
    from concourse.bass_utils import run_bass_kernel_spmd

    nc = bacc.Bacc("TRN2", target_bir_lowering=False, num_devices=1)
    arrays, d = {}, {}
    for name, a in layout({k: np.asarray(v) for k, v in inputs.items()}).items():
        a = np.ascontiguousarray(a)
        arrays[name] = a
        d[name] = nc.dram_tensor(name, a.shape, mybir.dt.from_np(a.dtype), kind="ExternalInput").ap()
    tokens = "s (t p) c -> p (s t) c"
    d["x"] = d["x"].rearrange(tokens, p=P)
    out = nc.dram_tensor("out", (NB, TB, C), F32, kind="ExternalOutput").ap()
    program(nc, d, out.rearrange(tokens, p=P))
    return run_bass_kernel_spmd(nc, [arrays], core_ids=[0]).results[0]["out"]
```
